# Optimizing a Trainium2 kernel written in Bass

```python
import numpy as np
import jax
import jax.numpy as jnp

def _softmax(x, axis=-1):
    return jax.nn.softmax(x, axis=axis)

def _gelu(x):
    return jax.nn.gelu(x, approximate=True)

def _silu(x):
    return jax.nn.silu(x)

def _sigmoid(x):
    return jax.nn.sigmoid(x)

def _layernorm(x, axis=-1, eps=1e-05):
    m = jnp.mean(x, axis=axis, keepdims=True)
    v = jnp.var(x, axis=axis, keepdims=True)
    return (x - m) / jnp.sqrt(v + eps)

def _scatter_add(tgt, idx, src, axis=0):
    return tgt.at[idx].add(src)

def _segment_sum(src, seg, n):
    return jax.ops.segment_sum(src, seg, n)
kernel_name = 'mk_xattn_seq_d2_seqx_r4_a64215'

def setup_inputs(seed: int=0):
    np.random.seed(seed)
    _w = jnp.asarray

    def _rec_inputs():
        import jax
        import jax.numpy as jnp
        _rk = jax.random.key(seed)
        x = -0.000125 + 0.9999 * jax.random.normal(jax.random.fold_in(_rk, 1), (4, 1024, 256), jnp.float32)
        _lenS = 1024 - jax.random.randint(jax.random.fold_in(_rk, 7), (4,), 0, max(1, 1024 // 4) + 1, jnp.int32)
        _lenS2 = 77 - jax.random.randint(jax.random.fold_in(_rk, 8), (4,), 0, max(1, 77 // 4) + 1, jnp.int32)
        _ctx_1024P = jax.random.normal(jax.random.fold_in(_rk, 11), (4, 16, 256), jnp.float32)
        _ctx_1024c = jax.random.dirichlet(jax.random.fold_in(_rk, 511), 0.3 * jnp.ones((16,), jnp.float32), (4, 77))
        _ctx_1024t = jnp.einsum('bsk,bkd->bsd', _ctx_1024c, _ctx_1024P)
        _ctx_1024t = _ctx_1024t * jax.lax.rsqrt(jnp.mean(jnp.square(_ctx_1024t)) + 1e-12) * 0.953939
        ctx_1024 = -1.52775e-05 + 0.999936 * (_ctx_1024t + 0.3 * jax.random.normal(jax.random.fold_in(_rk, 611), (4, 77, 256), jnp.float32))
        fside_Bx16xSxS2_0 = -1.47943e-05 + 1.00017 * jax.random.normal(jax.random.fold_in(_rk, 12), (4, 16, 1024, 77), jnp.float32)
        return (x, ctx_1024, fside_Bx16xSxS2_0)
    x, ctx_1024, fside_Bx16xSxS2_0 = _rec_inputs()

    def _L0_xattn_setup():
        import jax, jax.numpy as jnp
        import numpy as np
        B, N, D = (16, 512, 256)

        def _linear_params(key, d, scale):
            kw, kb = jax.random.split(key)
            W = jax.random.uniform(kw, (d, d), jnp.float32, -scale, scale)
            b = jax.random.uniform(kb, (d,), jnp.float32, -scale, scale)
            return (W, b)
        key = jax.random.key(seed)
        ks = jax.random.split(key, 9)
        scale = 1.0 / np.sqrt(D)
        x1 = jax.random.normal(ks[0], (B, N, D), jnp.float32)
        x2 = jax.random.normal(ks[1], (B, N, D), jnp.float32)
        Wq, bq = _linear_params(ks[2], D, scale)
        Wk, bk = _linear_params(ks[3], D, scale)
        Wv, bv = _linear_params(ks[4], D, scale)
        W1, b1 = _linear_params(ks[5], D, scale)
        W2, b2 = _linear_params(ks[6], D, scale)
        W3, b3 = _linear_params(ks[7], D, scale)
        gamma = jax.random.normal(ks[8], (1,), jnp.float32) * 0.1
        return {'x1': x1, 'x2': x2, 'Wq': Wq, 'bq': bq, 'Wk': Wk, 'bk': bk, 'Wv': Wv, 'bv': bv, 'W1': W1, 'b1': b1, 'W2': W2, 'b2': b2, 'W3': W3, 'b3': b3, 'gamma': gamma}
    _L0_xattn_all = _L0_xattn_setup()
    _L0_xattn_in = {k: v for k, v in _L0_xattn_all.items() if k in ('Wq', 'bq', 'Wk', 'bk', 'Wv', 'bv', 'W1', 'b1', 'W2', 'b2', 'W3', 'b3', 'gamma')}
    del _L0_xattn_all

    def _L1_xattn_setup():
        import jax, jax.numpy as jnp
        import numpy as np
        N_HEADS = 16
        D_MODEL = 256
        D_K = 64
        D_V = 64
        LN_EPS = 1e-06
        key = jax.random.key(seed)
        ks = jax.random.split(key, 16)
        B, L, D = (4, 128, D_MODEL)
        s = 1.0 / np.sqrt(D)
        return {'q': jax.random.normal(ks[0], (B, L, D), jnp.float32), 'k': jax.random.normal(ks[1], (B, L, D), jnp.float32), 'v': jax.random.normal(ks[2], (B, L, D), jnp.float32), 'bias': jax.random.normal(ks[3], (B, N_HEADS, L, L), jnp.float32), 'graph_attn_bias': jax.random.normal(ks[4], (B, N_HEADS, L, L), jnp.float32), 'wq': jax.random.normal(ks[5], (D, N_HEADS * D_K), jnp.float32) * s, 'bq': jnp.zeros((N_HEADS * D_K,), jnp.float32), 'wk': jax.random.normal(ks[6], (D, N_HEADS * D_K), jnp.float32) * s, 'bk': jnp.zeros((N_HEADS * D_K,), jnp.float32), 'wv': jax.random.normal(ks[7], (D, N_HEADS * D_V), jnp.float32) * s, 'bv': jnp.zeros((N_HEADS * D_V,), jnp.float32), 'wo': jax.random.normal(ks[8], (N_HEADS * D_V, D), jnp.float32) * s, 'bo': jnp.zeros((D,), jnp.float32), 'ln_g': jnp.ones((D,), jnp.float32), 'ln_b': jnp.zeros((D,), jnp.float32)}
    _L1_xattn_all = _L1_xattn_setup()
    _L1_xattn_in = {k: v for k, v in _L1_xattn_all.items() if k in ('wq', 'bq', 'wk', 'bk', 'wv', 'bv', 'wo', 'bo', 'ln_g', 'ln_b')}
    del _L1_xattn_all
    return {'x': x, 'ctx_1024': ctx_1024, 'fside_Bx16xSxS2_0': fside_Bx16xSxS2_0, 'L0_xattn_Wq': _L0_xattn_in['Wq'], 'L0_xattn_bq': _L0_xattn_in['bq'], 'L0_xattn_Wk': _L0_xattn_in['Wk'], 'L0_xattn_bk': _L0_xattn_in['bk'], 'L0_xattn_Wv': _L0_xattn_in['Wv'], 'L0_xattn_bv': _L0_xattn_in['bv'], 'L0_xattn_W1': _L0_xattn_in['W1'], 'L0_xattn_b1': _L0_xattn_in['b1'], 'L0_xattn_W2': _L0_xattn_in['W2'], 'L0_xattn_b2': _L0_xattn_in['b2'], 'L0_xattn_W3': _L0_xattn_in['W3'], 'L0_xattn_b3': _L0_xattn_in['b3'], 'L0_xattn_gamma': _L0_xattn_in['gamma'], 'L1_xattn_wq': _L1_xattn_in['wq'], 'L1_xattn_bq': _L1_xattn_in['bq'], 'L1_xattn_wk': _L1_xattn_in['wk'], 'L1_xattn_bk': _L1_xattn_in['bk'], 'L1_xattn_wv': _L1_xattn_in['wv'], 'L1_xattn_bv': _L1_xattn_in['bv'], 'L1_xattn_wo': _L1_xattn_in['wo'], 'L1_xattn_bo': _L1_xattn_in['bo'], 'L1_xattn_ln_g': _L1_xattn_in['ln_g'], 'L1_xattn_ln_b': _L1_xattn_in['ln_b']}

def reference(x, ctx_1024, fside_Bx16xSxS2_0, L0_xattn_Wq, L0_xattn_bq, L0_xattn_Wk, L0_xattn_bk, L0_xattn_Wv, L0_xattn_bv, L0_xattn_W1, L0_xattn_b1, L0_xattn_W2, L0_xattn_b2, L0_xattn_W3, L0_xattn_b3, L0_xattn_gamma, L1_xattn_wq, L1_xattn_bq, L1_xattn_wk, L1_xattn_bk, L1_xattn_wv, L1_xattn_bv, L1_xattn_wo, L1_xattn_bo, L1_xattn_ln_g, L1_xattn_ln_b):
    import jax
    import jax.numpy as jnp

    def _L0_xattn_ref(x1, x2, Wq, bq, Wk, bk, Wv, bv, W1, b1, W2, b2, W3, b3, gamma):
        import jax, jax.numpy as jnp
        import numpy as np
        B, N, D = (16, 512, 256)

        def _linear_params(key, d, scale):
            kw, kb = jax.random.split(key)
            W = jax.random.uniform(kw, (d, d), jnp.float32, -scale, scale)
            b = jax.random.uniform(kb, (d,), jnp.float32, -scale, scale)
            return (W, b)
        q = jnp.einsum('bnd,ed->bne', x1, Wq) + bq
        k = jnp.einsum('bnd,ed->bne', x2, Wk) + bk
        v = jnp.einsum('bnd,ed->bne', x2, Wv) + bv
        energy = jnp.einsum('bik,bjk->bij', q, k)
        attn = jax.nn.softmax(energy, axis=-1)
        out = jnp.einsum('bij,bjk->bik', attn, v)
        s = jnp.einsum('bnd,ed->bne', out, W1) + b1 + jnp.einsum('bnd,ed->bne', out, W2) + b2 + jnp.einsum('bnd,ed->bne', out, W3) + b3
        out = out * jax.nn.sigmoid(s)
        return gamma * out + x1

    def _L1_xattn_ref(q, k, v, bias, graph_attn_bias, wq, bq, wk, bk, wv, bv, wo, bo, ln_g, ln_b):
        import jax, jax.numpy as jnp
        import numpy as np
        N_HEADS = 16
        D_MODEL = 256
        D_K = 64
        D_V = 64
        LN_EPS = 1e-06
        B, Lq, D = q.shape
        H, dk, dv = (N_HEADS, D_K, D_V)
        residual = q
        qh = (q @ wq + bq).reshape(B, Lq, H, dk).transpose(0, 2, 1, 3)
        kh = (k @ wk + bk).reshape(B, k.shape[1], H, dk).transpose(0, 2, 1, 3)
        vh = (v @ wv + bv).reshape(B, v.shape[1], H, dv).transpose(0, 2, 1, 3)
        scores = jnp.einsum('bhqd,bhkd->bhqk', qh / np.sqrt(dk).astype(qh.dtype), kh)
        scores = scores + bias + graph_attn_bias
        weights = jax.nn.softmax(scores, axis=-1)
        ctx = jnp.einsum('bhqk,bhkd->bhqd', weights, vh)
        ctx = ctx.transpose(0, 2, 1, 3).reshape(B, Lq, H * dv)
        out = ctx @ wo + bo + residual
        mu = jnp.mean(out, axis=-1, keepdims=True)
        var = jnp.var(out, axis=-1, keepdims=True)
        out = (out - mu) * jax.lax.rsqrt(var + LN_EPS) * ln_g + ln_b
        return out
    x = _L0_xattn_ref(x, ctx_1024, L0_xattn_Wq, L0_xattn_bq, L0_xattn_Wk, L0_xattn_bk, L0_xattn_Wv, L0_xattn_bv, L0_xattn_W1, L0_xattn_b1, L0_xattn_W2, L0_xattn_b2, L0_xattn_W3, L0_xattn_b3, L0_xattn_gamma)
    x = _L1_xattn_ref(x, ctx_1024, ctx_1024, fside_Bx16xSxS2_0, fside_Bx16xSxS2_0, L1_xattn_wq, L1_xattn_bq, L1_xattn_wk, L1_xattn_bk, L1_xattn_wv, L1_xattn_bv, L1_xattn_wo, L1_xattn_bo, L1_xattn_ln_g, L1_xattn_ln_b)
    return x

_drawn_inputs = setup_inputs


def setup_inputs(seed=0):
    import zlib

    import numpy as np

    out = dict(_drawn_inputs(seed))
    spreads = {'L1_xattn_bq': (0.0, 0.1),
     'L1_xattn_bk': (0.0, 2.0),
     'L1_xattn_bv': (0.0, 0.1),
     'L1_xattn_bo': (0.0, 0.1),
     'L1_xattn_ln_g': (1.0, 0.2),
     'L1_xattn_ln_b': (0.0, 0.1)}
    factors = {'L0_xattn_Wq': 4.978,
     'L0_xattn_bq': 8.0,
     'L0_xattn_Wk': 4.965,
     'L0_xattn_bk': 200.0,
     'L0_xattn_Wv': 4.23,
     'L0_xattn_bv': 26.144,
     'L0_xattn_W1': 8.0,
     'L0_xattn_b1': 200.0,
     'L0_xattn_W2': 8.0,
     'L0_xattn_b2': 200.0,
     'L0_xattn_W3': 8.0,
     'L0_xattn_b3': 200.0}
    for name, (base, spread) in spreads.items():
        noise = np.random.default_rng([zlib.crc32(name.encode()), seed]).standard_normal(out[name].shape)
        drawn = base * np.exp(spread * noise) if base else spread * noise
        out[name] = jnp.asarray(drawn.astype(out[name].dtype))
    for name, factor in factors.items():
        out[name] = (out[name] * factor).astype(out[name].dtype)
    return out
```

```python
from contextlib import ExitStack

import concourse.bass as bass
from concourse import mybir

F32 = mybir.dt.float32
F32R = mybir.dt.float32r
ALU = mybir.AluOpType
ACT = mybir.ActivationFunctionType
AX = mybir.AxisListType

P = 128
NB, SEQ, D = 4, 1024, 256
KEYS, HEADS, DK = 77, 16, 64
DC = D // P
TILES = SEQ // P
GROUP = 4
GROUPS = TILES // GROUP
PAIRS = HEADS // 2
HK = HEADS * KEYS
HKP = -(-HK // P) * P
CH = HKP // P
PW = 2 * KEYS
AK = NB * KEYS
BANK = 512
SCORE_PAIRS = [(0, 3), (3, 6), (6, 8)]
SCORE_COLS = [(a * PW, b * PW) for a, b in SCORE_PAIRS]
PT_FILLS = [(0, 4), (4, 8), (8, 10)]
PT_BANK = [0, 1, 0]
HALVES = [(0, HEADS // 2), (HEADS // 2, HEADS)]
SLOTS = 4
YSLOTS = 4
VSTRIDE = P + PW
VWIDTH = P + PAIRS * VSTRIDE
SCALE = DK ** -0.5
EPS = 1e-6
VO_FILLS = CH // 2
X1T_LAG = 2
VO_IN_STEP = [range(0, 3), range(3, VO_FILLS)]
assert SCALE == 0.125 and CH == PT_FILLS[-1][1]
C_BK0, C_BV0, C_BQ0, C_BQ1, C_BK1, C_BV1 = 0, 2, 4, 6, 14, 22
NCOLS = 30
R_BV0, R_B1, R_B2, R_B3, R_LNG, R_LNB = range(6)


def build(nc, x, xT, cT, fside, wq0, wk0T, wv0T, w1T, w2T, w3T, wqT, wk, wv, wo, cols, rows, bo, gamma, ident_in, out):
    x_v = x.rearrange("(b g i p) d -> p b g i d", b=NB, g=GROUPS, i=GROUP)
    xT_v = xT.rearrange("(c p) n -> p c n", p=P)
    f_v = fside.rearrange("(t p) n -> p t n", p=P)
    out_v = out.rearrange("(t p) n -> p t n", p=P)

    with ExitStack() as ctx:
        def sb(name, shape, dt=F32):
            return ctx.enter_context(nc.sbuf_tensor(name, shape, dt))

        def sem(name):
            return ctx.enter_context(nc.semaphore(name))

        wqT_sb = sb("wqT_sb", [P, PAIRS, D])
        wo_sb = sb("wo_sb", [P, PAIRS, D])
        kh_all = sb("kh_all", [P, PAIRS, AK])
        vh_all = sb("vh_all", [P, PAIRS, AK])
        bq_rep = sb("bq_rep", [P, PAIRS, P])
        m_all = sb("m_all", [P, DC, (NB - 1) * KEYS + P])
        rb0 = sb("rb0", [P, AK])
        vvs_hi = sb("vvs_hi", [P, NB * BANK], F32R)
        vvs_lo = sb("vvs_lo", [P, NB * BANK], F32R)
        ln_gb = sb("ln_gb", [P, 2, D])
        ident = sb("ident", [P, P])
        cols_sb = sb("cols_sb", [P, NCOLS])
        small = sb("small", [P, 8])
        bk8 = sb("bk8", [P, PAIRS])
        bo_sb = sb("bo_sb", [1, D])
        sel_h0 = sb("sel_h0", [1, P])
        blk_k = sb("blk_k", [P, PAIRS * PW])
        blk_v = sb("blk_v", [P, VWIDTH])
        g_hi = sb("g_hi", [P, DC, HK], F32R)
        g_lo = sb("g_lo", [P, DC, HK], F32R)
        vo_hi = sb("vo_hi", [P, CH, D], F32R)
        vo_lo = sb("vo_lo", [P, CH, D], F32R)
        rb1 = sb("rb1", [P, HK])
        fs = sb("fs", [P, SLOTS * HKP])
        pt_hi = sb("pt_hi", [P, CH, P], F32R)
        pt_lo = sb("pt_lo", [P, CH, P], F32R)
        x1T_hi = sb("x1T_hi", [P, TILES, D], F32R)
        x1T_lo = sb("x1T_lo", [P, TILES, D], F32R)
        xrow = sb("xrow", [P, TILES * D])
        xT_sb = sb("xT_sb", [P, DC, SEQ])
        attn = sb("attn", [P, TILES * P])
        aT_hi = sb("aT_hi", [P, TILES, P], F32R)
        aT_lo = sb("aT_lo", [P, TILES, P], F32R)
        work = sb("work", [P, (YSLOTS + 4) * D])
        y = work[:, 0:YSLOTS * D].rearrange("p (s d) -> p s d", s=YSLOTS)
        th = work[:, YSLOTS * D:(YSLOTS + 2) * D].rearrange("p (s d) -> p s d", s=2)
        o_sb = work[:, (YSLOTS + 2) * D:(YSLOTS + 4) * D].rearrange("p (s d) -> p s d", s=2)
        negmax = sb("negmax", [P, 2, HEADS])
        sums = sb("sums", [P, 2, HEADS])
        rsum = sb("rsum", [P, 2, HEADS])
        negmax0 = sb("negmax0", [P, TILES])
        sums0 = sb("sums0", [P, TILES])
        rsum0 = sb("rsum0", [P, TILES])
        stats = sb("stats", [P, 6])
        meanvar = sb("meanvar", [P, YSLOTS, 2])
        var_eps = sb("var_eps", [P, YSLOTS])
        rstd = sb("rstd", [P, YSLOTS])

        wk_sb = fs[:, 0:DC * HEADS * DK].rearrange("p (c n) -> p c n", c=DC)
        wv_sb = fs[:, DC * HEADS * DK:2 * DC * HEADS * DK].rearrange("p (c n) -> p c n", c=DC)
        w123 = xrow[:, 0:3 * DC * D].rearrange("p (w n) -> p w n", w=3)
        wsum = attn[:, 0:DC * D]
        wk0_sb = work[:, 0:DC * D].rearrange("p (c n) -> p c n", c=DC)
        wv0_sb = work[:, DC * D:2 * DC * D].rearrange("p (c n) -> p c n", c=DC)
        wq0_sb = work[:, 2 * DC * D:3 * DC * D].rearrange("p (c n) -> p c n", c=DC)
        vvs_raw = work[:, 3 * DC * D:3 * DC * D + BANK]
        kT0 = blk_v[:, 0:DC * AK].rearrange("p (c n) -> p c n", c=DC)
        vT0 = blk_v[:, DC * AK:2 * DC * AK].rearrange("p (c n) -> p c n", c=DC)
        cT_sb = rb1[:, 0:DC * AK].rearrange("p (c n) -> p c n", c=DC)
        bias_rows = blk_k[:, 0:4 * D].rearrange("p (r d) -> p r d", r=4)
        bq0_rep = rb1[:, DC * AK:DC * AK + DC * P].rearrange("p (c n) -> p c n", c=DC)

        ps = [ctx.enter_context(nc.psum_tensor(f"bank{i}", [P, BANK], F32)) for i in range(8)]
        S_BANK, T_BANK, O_BANK, E_BANK, X_BANK = ps[0:3], ps[3:5], ps[5], ps[6], ps[7]
        L0_BANK = [E_BANK, X_BANK]
        GATE_BANK = [E_BANK, X_BANK, S_BANK[1], S_BANK[2]]
        X1T_BANK = [O_BANK, T_BANK[1], S_BANK[0]]
        NG, NX = len(GATE_BANK), len(X1T_BANK)

        ld_ctx, ld_w0, ld_wkv, ld_w123, ld_vec, ld_w1 = (sem(f"ld_{n}") for n in ("ctx", "w0", "wkv", "w123", "vec", "w1"))
        f_loaded = [sem(f"f_loaded{i}") for i in range(SLOTS)]
        xT_loaded = sem("xT_loaded")
        x_loaded = [sem(f"x_loaded{g}") for g in range(GROUPS)]
        out_stored = [sem(f"out_stored{i}") for i in range(YSLOTS)]
        consts_set, wsum_ready, su_filled, su_act, su_dve = (sem(n) for n in ("consts_set", "wsum_ready", "su_filled", "su_act", "su_dve"))
        vvs_step, pads_set = sem("vvs_step"), sem("pads_set")
        vvs_chain, pool_chain = sem("vvs_chain"), sem("pool_chain")
        energy_filled, g_filled, rb_filled, attnT_filled = (sem(n) for n in ("energy_filled", "g_filled", "rb_filled", "attnT_filled"))
        l0_filled, x1T_filled, vo_filled = (sem(n) for n in ("l0_filled", "x1T_filled", "vo_filled"))
        scores_filled, pT_filled, out_filled = (sem(n) for n in ("scores_filled", "pT_filled", "out_filled"))
        blk_k_ready, g_hi_ready, exp0_done, aT_hi_ready = (sem(n) for n in ("blk_k_ready", "g_hi_ready", "exp0_done", "aT_hi_ready"))
        tanh_ready, x1T_hi_ready, vo_hi_ready, pT_hi_ready, exp_done = (sem(n) for n in ("tanh_ready", "x1T_hi_ready", "vo_hi_ready", "pT_hi_ready", "exp_done"))
        blk_v_ready, e_biased, negmax0_ready, rsum0_ready, g_lo_ready = (sem(n) for n in ("blk_v_ready", "e_biased", "negmax0_ready", "rsum0_ready", "g_lo_ready"))
        rb1_ready, aT_lo_ready, gated, x1T_lo_ready, vo_lo_ready = (sem(n) for n in ("rb1_ready", "aT_lo_ready", "gated", "x1T_lo_ready", "vo_lo_ready"))
        s_biased, negmax_ready, rsum_ready, pT_lo_ready = (sem(n) for n in ("s_biased", "negmax_ready", "rsum_ready", "pT_lo_ready"))
        y_summed, y_stats, y_meanvar, var_ready, y_normed = (sem(n) for n in ("y_summed", "y_stats", "y_meanvar", "var_ready", "y_normed"))
        attn_ready, x1_ready, f_biased, probs_ready = (sem(n) for n in ("attn_ready", "x1_ready", "f_biased", "probs_ready"))
        rstd_ready, y_scaled, y_final = (sem(n) for n in ("rstd_ready", "y_scaled", "y_final"))

        def f_slot(s, a=0, b=HK):
            return fs[:, (s % SLOTS) * HKP + a:(s % SLOTS) * HKP + b]

        SETUP = ([("kT0", i, "act") for i in range(DC)] + [("vT0", i, "dve") for i in range(DC)]
                 + [kv for j in range(PAIRS) for kv in (("kh", j, "act"), ("vh", j, "dve"))]
                 + [("m", i, "act") for i in range(DC)] + [("rb0", 0, "dve")] + [("vvs", b, "dve") for b in range(NB)])
        N_SETUP = len(SETUP)
        N_PADS_EARLY, N_PADS = 5, 9
        HEAD_WEIGHTS_USED = 2 * DC + 2 * PAIRS

        def evacuated(i):
            who = SETUP[i][2]
            return (su_act if who == "act" else su_dve), sum(w == who for _, _, w in SETUP[:i + 1])

        block = ctx.enter_context(nc.Block())

        @block.sync
        def _(sp):
            def load_xT(b):
                sp.dma_start(xT_sb[:, :, :], xT_v[:, :, bass.ds(b * SEQ, SEQ)]).then_inc(xT_loaded, 16)

            def load_x(b, g):
                sp.dma_start(xrow[:, g * GROUP * D:(g + 1) * GROUP * D].rearrange("p (i d) -> p i d", i=GROUP),
                             x_v[:, bass.ds(b, 1), g, :, :].rearrange("p b i d -> p (b i) d")).then_inc(x_loaded[g], 16)

            def load_f(b, s):
                sp.dma_start(f_slot(s), f_v[:, bass.ds(b * TILES + s, 1), :].rearrange("p t n -> p (t n)")).then_inc(f_loaded[s % SLOTS], 16)

            def store(b, s):
                sp.wait_ge(y_final, b * TILES + s + 1)
                sp.dma_start(out_v[:, bass.ds(b * TILES + s, 1), :].rearrange("p t n -> p (t n)"),
                             y[:, s % YSLOTS, :]).then_inc(out_stored[s % YSLOTS], 16)

            def batch(b, first, last):
                if not first:
                    store(b - 1, 5)
                    store(b - 1, 6)
                    sp.wait_ge(y_summed, b * TILES)
                    load_x(b, 1)
                    store(b - 1, 7)
                for s in range(TILES):
                    if s >= 2:
                        sp.wait_ge(pT_filled, 3 * (b * TILES + s - 1))
                        if s + 2 < TILES:
                            load_f(b, s + 2)
                        elif not last:
                            load_f(b + 1, s + 2 - TILES)
                    elif s + 2 < TILES:
                        if not first:
                            sp.wait_ge(pT_filled, 3 * (b * TILES + s - 1))
                        load_f(b, s + 2)
                    if s == 0 and not last:
                        sp.wait_ge(energy_filled, GROUPS * (b + 1))
                        load_xT(b + 1)
                    if s >= 3:
                        store(b, s - 3)
                    if s == 6 and not last:
                        sp.wait_ge(y_summed, b * TILES + 4)
                        load_x(b + 1, 0)

            sp.dma_start(cT_sb, cT.rearrange("(c p) n -> p c n", p=P)).then_inc(ld_ctx, 16)
            sp.dma_start(wk0_sb, wk0T.rearrange("(c p) n -> p c n", p=P)).then_inc(ld_w0, 16)
            sp.dma_start(wv0_sb, wv0T.rearrange("(c p) n -> p c n", p=P)).then_inc(ld_w0, 16)
            sp.dma_start(wk_sb, wk.rearrange("(c p) n -> p c n", p=P)).then_inc(ld_wkv, 16)
            sp.dma_start(wv_sb, wv.rearrange("(c p) n -> p c n", p=P)).then_inc(ld_wkv, 16)
            sp.dma_start(wq0_sb, wq0.rearrange("(c p) n -> p c n", p=P)).then_inc(ld_w0, 16)
            for i, w in enumerate((w1T, w2T, w3T)):
                sp.dma_start(w123[:, i, :].rearrange("p (c n) -> p c n", c=DC), w.rearrange("(c p) n -> p c n", p=P)).then_inc(ld_w123, 16)
            load_xT(0)
            sp.dma_start(wqT_sb[:, :, :], wqT.rearrange("(c p) n -> p c n", p=P)).then_inc(ld_w1, 16)
            sp.dma_start(wo_sb[:, :, :], wo.rearrange("(c p) n -> p c n", p=P)).then_inc(ld_w1, 16)
            sp.wait_ge(wsum_ready, 2)
            load_x(0, 0)
            load_x(0, 1)
            sp.wait_ge(su_filled, HEAD_WEIGHTS_USED)
            load_f(0, 0)
            load_f(0, 1)
            batch(0, True, False)
            with sp.Fori(1, NB - 1) as b:
                batch(b, False, False)
            batch(NB - 1, False, True)
            for s in (5, 6, 7):
                store(NB - 1, s)
            for i in range(YSLOTS):
                sp.wait_ge(out_stored[i], 16 * NB * TILES // YSLOTS)

        @block.tensor
        def _(pe):
            mm = nc.tensor.matmul

            def three_pass(dst, a_hi, a_lo, b_hi, b_lo, start, stop):
                mm(dst, a_hi, b_hi, start=start, stop=False)
                mm(dst, a_hi, b_lo, start=False, stop=False)
                return mm(dst, a_lo, b_hi, start=False, stop=stop)

            def setup():
                pe.wait_ge(ld_ctx, 16)
                pe.wait_ge(ld_w0, 48)
                for i, (what, n, _) in enumerate(SETUP):
                    if i >= 8:
                        pe.wait_ge(*evacuated(i - 8))
                    dst = ps[i % 8]
                    if what == "kh" and n == 0:
                        pe.wait_ge(ld_wkv, 32)
                    if what == "m" and n == 0:
                        pe.wait_ge(*evacuated(DC - 1))
                    if what == "rb0":
                        pe.wait_ge(consts_set, 1)
                    if what == "vvs" and n == 0:
                        pe.wait_ge(*evacuated(2 * DC - 1))
                        pe.wait_ge(wsum_ready, 2)
                    for c in range(DC):
                        first, last = c == 0, c == DC - 1
                        if what == "kT0":
                            ins = mm(dst[:, 0:AK], wk0_sb[:, c, n * P:(n + 1) * P], cT_sb[:, c, :], start=first, stop=last)
                        elif what == "vT0":
                            ins = mm(dst[:, 0:AK], wv0_sb[:, c, n * P:(n + 1) * P], cT_sb[:, c, :], start=first, stop=last)
                        elif what == "kh":
                            ins = mm(dst[:, 0:AK], wk_sb[:, c, n * P:(n + 1) * P], cT_sb[:, c, :], start=first, stop=last)
                        elif what == "vh":
                            ins = mm(dst[:, 0:AK], wv_sb[:, c, n * P:(n + 1) * P], cT_sb[:, c, :], start=first, stop=last)
                        elif what == "m":
                            ins = mm(dst[:, 0:AK], wq0_sb[:, c, n * P:(n + 1) * P], kT0[:, c, :], start=first, stop=last)
                        elif what == "rb0":
                            ins = mm(dst[:, 0:AK], bq0_rep[:, c, :], kT0[:, c, :], start=first, stop=last)
                        elif what == "vvs":
                            ins = mm(dst[0:KEYS, 0:D], cT_sb[:, c, n * KEYS:(n + 1) * KEYS], wv0_sb[:, c, :], start=first, stop=last)
                    if what == "vvs":
                        for c in range(DC):
                            ins = mm(dst[0:KEYS, D:2 * D], vT0[:, c, n * KEYS:(n + 1) * KEYS], wsum[:, c * D:(c + 1) * D],
                                     start=c == 0, stop=c == DC - 1)
                    ins.then_inc(su_filled, 1)

            def energy(b, g, prev):
                if prev:
                    pe.wait_ge(gated, b * TILES - NG + 1 + g)
                for i in range(GROUP):
                    for c in range(DC):
                        ins = mm(L0_BANK[g][:, i * P:(i + 1) * P], xT_sb[:, c, (g * GROUP + i) * P:(g * GROUP + i + 1) * P],
                                 m_all[:, c, bass.ds(b * KEYS, P)], start=c == 0, stop=c == DC - 1)
                ins.then_inc(energy_filled, 1)

            def g_fill(b, n, prev):
                c, k = n // 3, n % 3
                if c == 0 and prev:
                    pe.wait_ge(s_biased, 3 * b * TILES - 2 + k)
                elif c:
                    pe.wait_ge(g_lo_ready, b * 6 + n - 2)
                a, e = SCORE_PAIRS[k]
                for pr in range(a, e):
                    ins = mm(S_BANK[k][:, (pr - a) * PW:(pr - a + 1) * PW], wqT_sb[:, pr, c * P:(c + 1) * P],
                             blk_k[:, pr * PW:(pr + 1) * PW], start=True, stop=True)
                ins.then_inc(g_filled, 1)

            def rb_fill(b, k):
                pe.wait_ge(g_lo_ready, b * 6 + 4 + k)
                a, e = SCORE_PAIRS[k]
                for pr in range(a, e):
                    ins = mm(S_BANK[k][:, (pr - a) * PW:(pr - a + 1) * PW], bq_rep[:, pr, :],
                             blk_k[:, pr * PW:(pr + 1) * PW], start=True, stop=True)
                ins.then_inc(rb_filled, 1)

            def attnT(b, g):
                pe.wait_ge(e_biased, b * GROUPS + g + 1)
                pe.wait_ge(attn_ready, b * GROUPS + g + 1)
                for i in range(GROUP):
                    ins = nc.tensor.transpose(L0_BANK[g][:, i * P:(i + 1) * P], attn[:, (g * GROUP + i) * P:(g * GROUP + i + 1) * P], ident[:, :])
                ins.then_inc(attnT_filled, 1)

            def l0_out(b, i):
                if i % GROUP == 0:
                    pe.wait_ge(aT_lo_ready, b * GROUPS + i // GROUP + 1)
                if i == 1:
                    pe.wait_ge(aT_lo_ready, b * GROUPS + 2)
                elif i in (2, 3):
                    pe.wait_ge(rb1_ready, 3 * b + i)
                elif i >= NG:
                    pe.wait_ge(gated, b * TILES + i - NG + 1)
                v = bass.ds(b * BANK, BANK)
                three_pass(GATE_BANK[i % NG][:, :], aT_hi[:, i, :], aT_lo[:, i, :], vvs_hi[:, v], vvs_lo[:, v], True, True).then_inc(l0_filled, 1)

            def x1T(b, i, prev):
                pe.wait_ge(x1_ready, b * TILES + i + 1)
                if i >= NX:
                    pe.wait_ge(x1T_lo_ready, b * TILES + i - NX + 1)
                elif i == 2:
                    pe.wait_ge(rb1_ready, 3 * b + 1)
                elif prev and i == 0:
                    pe.wait_ge(y_summed, b * TILES)
                elif prev:
                    pe.wait_ge(pT_lo_ready, 3 * b * TILES - 1)
                for c in range(DC):
                    ins = nc.tensor.transpose(X1T_BANK[i % NX][:, c * P:(c + 1) * P], xrow[:, i * D + c * P:i * D + (c + 1) * P], ident[:, :])
                ins.then_inc(x1T_filled, 1)

            def vo_fill(b, n, prev):
                if n == 0:
                    pe.wait_ge(blk_v_ready, b + 1)
                    if prev:
                        pe.wait_ge(pT_lo_ready, 3 * b * TILES)
                elif n == 1:
                    pe.wait_ge(x1T_lo_ready, (b + 1) * TILES)
                else:
                    pe.wait_ge(vo_lo_ready, b * VO_FILLS + n - 1)
                for half in range(2):
                    c = 2 * n + half
                    dst = T_BANK[n % 2][:, half * D:(half + 1) * D]
                    pairs = [pr for pr in range(PAIRS) if pr * PW < (c + 1) * P and (pr + 1) * PW > c * P]
                    for pr in pairs:
                        at = P + pr * VSTRIDE + c * P - pr * PW
                        ins = mm(dst, blk_v[:, at:at + P], wo_sb[:, pr, :], start=pr == pairs[0], stop=c > 0 and pr == pairs[-1])
                    if c == 0:
                        ins = mm(dst, sel_h0[:, :], bo_sb[:, :], start=False, stop=True)
                ins.then_inc(vo_filled, 1)

            def scores(b, s, k, first_tile_of_batch):
                if k == 0:
                    pe.wait_ge(x1T_lo_ready, b * TILES + s + 1)
                if first_tile_of_batch:
                    if k == 0:
                        pe.wait_ge(g_lo_ready, (b + 1) * 6)
                        pe.wait_ge(x1T_lo_ready, (b + 1) * TILES)
                    else:
                        pe.wait_ge(gated, (b + 1) * TILES)
                else:
                    pe.wait_ge(s_biased, 3 * (b * TILES + s) - 2 + k)
                a, e = SCORE_COLS[k]
                for c in range(DC):
                    ins = three_pass(S_BANK[k][:, 0:e - a], x1T_hi[:, s, c * P:(c + 1) * P], x1T_lo[:, s, c * P:(c + 1) * P],
                                     g_hi[:, c, a:e], g_lo[:, c, a:e], c == 0, c == DC - 1)
                ins.then_inc(scores_filled, 1)

            def pT(b, s, k):
                at = 3 * (b * TILES + s)
                if k < 2:
                    pe.wait_ge(probs_ready, 2 * (b * TILES + s) + k + 1)
                if k == 2:
                    pe.wait_ge(pT_lo_ready, at + 1)
                elif s == 0 and k == 0:
                    pe.wait_ge(vo_lo_ready, (b + 1) * VO_FILLS)
                elif s > 0:
                    pe.wait_ge(pT_lo_ready, at - (0 if k == 0 else 1))
                c0, c1 = PT_FILLS[k]
                for c in range(c0, c1):
                    ins = nc.tensor.transpose(T_BANK[PT_BANK[k]][:, (c - c0) * P:(c - c0 + 1) * P],
                                              f_slot(s, c * P, (c + 1) * P), ident[:, :])
                ins.then_inc(pT_filled, 1)

            def pv(b, s, k):
                pe.wait_ge(pT_lo_ready, 3 * (b * TILES + s) + k + 1)
                if k == 0 and s == 0:
                    pe.wait_ge(x1T_lo_ready, (b + 1) * TILES)
                elif k == 0:
                    pe.wait_ge(y_summed, b * TILES + s)
                c0, c1 = PT_FILLS[k]
                for c in range(c0, c1):
                    ins = three_pass(O_BANK[:, 0:D], pt_hi[:, c, :], pt_lo[:, c, :], vo_hi[:, c, :], vo_lo[:, c, :], c == 0, c == CH - 1)
                if k == 2:
                    ins.then_inc(out_filled, 1)

            def head(b, prev, cur):
                if cur:
                    pe.wait_ge(xT_loaded, 16 * (b + 1))
                    energy(b, 0, prev)
                    energy(b, 1, prev)
                if prev:
                    pT(b - 1, 6, 0)
                    pT(b - 1, 6, 1)
                if cur:
                    pe.wait_ge(blk_k_ready, b + 1)
                    for n in range(3):
                        g_fill(b, n, prev)
                if prev:
                    pT(b - 1, 6, 2)
                if cur:
                    for n in range(3, 6):
                        g_fill(b, n, prev)
                if prev:
                    for k in range(3):
                        pv(b - 1, 6, k)
                if cur:
                    attnT(b, 0)
                if prev:
                    pT(b - 1, 7, 0)
                    pT(b - 1, 7, 1)
                if cur:
                    rb_fill(b, 0)
                    rb_fill(b, 1)
                if prev:
                    pT(b - 1, 7, 2)
                if cur:
                    rb_fill(b, 2)
                    attnT(b, 1)
                if prev:
                    for k in range(3):
                        pv(b - 1, 7, k)
                if cur:
                    for i in range(TILES + X1T_LAG):
                        if i < TILES:
                            l0_out(b, i)
                        if i >= X1T_LAG:
                            x1T(b, i - X1T_LAG, prev)

            def batch(b, prev):
                head(b, prev, True)
                for s in range(TILES):
                    if s < 2:
                        for k in range(3):
                            scores(b, s, k, s == 0)
                        for n in VO_IN_STEP[s]:
                            vo_fill(b, n, prev)
                        continue
                    pT(b, s - 2, 0)
                    scores(b, s, 0, False)
                    pT(b, s - 2, 1)
                    scores(b, s, 1, False)
                    pT(b, s - 2, 2)
                    pv(b, s - 2, 0)
                    scores(b, s, 2, False)
                    pv(b, s - 2, 1)
                    pv(b, s - 2, 2)

            setup()
            for who, i in (("act", 0), ("dve", 0)):
                last = max(n for n in range(N_SETUP) if SETUP[n][2] == who)
                pe.wait_ge(*evacuated(last))
            pe.wait_ge(vvs_step, 3 * NB)
            pe.wait_ge(pads_set, N_PADS)
            pe.wait_ge(ld_w1, 32)
            batch(0, False)
            with pe.Fori(1, NB) as b:
                batch(b, True)
            head(NB, True, False)

        @block.scalar
        def _(act):
            copy = nc.scalar.copy
            act.dma_start(ident[:, :], ident_in).then_inc(ld_vec, 16)
            act.dma_start(cols_sb[:, :], cols).then_inc(ld_vec, 16)
            act.dma_start(small[:, 0:1], gamma.partition_broadcast(P)).then_inc(ld_vec, 16)
            act.dma_start(bias_rows, rows[R_BV0:R_B3 + 1, :].partition_broadcast(P)).then_inc(ld_vec, 16)
            act.dma_start(ln_gb[:, :, :], rows[R_LNG:R_LNB + 1, :].partition_broadcast(P)).then_inc(ld_vec, 16)
            act.dma_start(bo_sb[:, :], bo).then_inc(ld_vec, 16)

            def setup():
                act.wait_ge(ld_vec, 96)
                for c in range(DC):
                    ins = copy(bq0_rep[:, c, :], cols_sb[:, C_BQ0 + c:C_BQ0 + c + 1].broadcast_to([P, P]))
                ins.then_inc(consts_set, 1)
                for pr in range(PAIRS):
                    copy(bq_rep[:, pr, :], cols_sb[:, C_BQ1 + pr:C_BQ1 + pr + 1].broadcast_to([P, P]))
                act.wait_ge(pads_set, N_PADS_EARLY)
                for i, (what, n, who) in enumerate(SETUP):
                    src = ps[i % 8][:, 0:AK]
                    if what == "vvs":
                        act.wait_ge(vvs_step, 3 * n + 1)
                        copy(vvs_hi[0:KEYS, n * BANK:(n + 1) * BANK], vvs_raw[0:KEYS, :]).then_inc(vvs_step, 1)
                        continue
                    if who != "act":
                        continue
                    act.wait_ge(su_filled, i + 1)
                    if what == "kT0":
                        ins = nc.scalar.activation(kT0[:, n, :], src, ACT.Identity, bias=cols_sb[:, C_BK0 + n:C_BK0 + n + 1])
                    elif what == "kh":
                        if n == 0:
                            act.wait_ge(wsum_ready, 1)
                        ins = nc.scalar.activation(kh_all[:, n, :], src, ACT.Identity, bias=bk8[:, n:n + 1], scale=SCALE)
                    else:
                        ins = copy(m_all[:, n, 0:AK], src)
                    ins.then_inc(su_act, 1)

            def blk_k_copy(b, prev):
                if prev:
                    act.wait_ge(rb_filled, 3 * b)
                view = blk_k[:, :].rearrange("p (r n) -> p r n", r=PAIRS)
                copy(view[0:DK, :, 0:KEYS], kh_all[0:DK, :, bass.ds(b * KEYS, KEYS)])
                copy(view[DK:P, :, KEYS:PW], kh_all[DK:P, :, bass.ds(b * KEYS, KEYS)]).then_inc(blk_k_ready, 1)

            def g_split(b, n):
                c, k = n // 3, n % 3
                a, e = SCORE_COLS[k]
                act.wait_ge(g_filled, b * 6 + n + 1)
                copy(g_hi[:, c, a:e], S_BANK[k][:, 0:e - a]).then_inc(g_hi_ready, 1)

            def vo_split(b, n):
                act.wait_ge(vo_filled, b * VO_FILLS + n + 1)
                copy(vo_hi[:, 2 * n:2 * n + 2, :].rearrange("p c n -> p (c n)"), T_BANK[n % 2][:, :]).then_inc(vo_hi_ready, 1)

            def exp0(b, g):
                act.wait_ge(negmax0_ready, b * GROUPS + g + 1)
                for i in range(g * GROUP, (g + 1) * GROUP):
                    e = attn[:, i * P:i * P + KEYS]
                    ins = nc.scalar.activation(e, e, ACT.Exp, bias=negmax0[:, i:i + 1], accum_out=sums0[:, i:i + 1])
                ins.then_inc(exp0_done, 1)

            def aT_split(b, g):
                act.wait_ge(attnT_filled, b * GROUPS + g + 1)
                copy(aT_hi[:, g * GROUP:(g + 1) * GROUP, :].rearrange("p i n -> p (i n)"), L0_BANK[g][:, :]).then_inc(aT_hi_ready, 1)

            def tanh(b, i):
                act.wait_ge(l0_filled, b * TILES + i + 1)
                if i >= 2:
                    act.wait_ge(gated, b * TILES + i - 1)
                nc.scalar.activation(th[:, i % 2, :], GATE_BANK[i % NG][:, D:2 * D], ACT.Tanh, scale=0.5).then_inc(tanh_ready, 1)

            def x1T_split(b, i):
                act.wait_ge(x1T_filled, b * TILES + i + 1)
                copy(x1T_hi[:, i, :], X1T_BANK[i % NX][:, 0:D]).then_inc(x1T_hi_ready, 1)

            def pT_split(b, s, k):
                c0, c1 = PT_FILLS[k]
                act.wait_ge(pT_filled, 3 * (b * TILES + s) + k + 1)
                copy(pt_hi[:, c0:c1, :].rearrange("p c n -> p (c n)"), T_BANK[PT_BANK[k]][:, 0:(c1 - c0) * P]).then_inc(pT_hi_ready, 1)

            def exp(b, s, h0, h1):
                if h0 == 0:
                    act.wait_ge(negmax_ready, b * TILES + s + 1)
                for h in range(h0, h1):
                    e = f_slot(s, h * KEYS, (h + 1) * KEYS)
                    ins = nc.scalar.activation(e, e, ACT.Exp, bias=negmax[:, s % 2, h:h + 1], accum_out=sums[:, s % 2, h:h + 1])
                    if h + 1 in (HALVES[0][1], HALVES[1][1]):
                        ins.then_inc(exp_done, 1)

            def head(b, prev, cur):
                if cur:
                    blk_k_copy(b, prev)
                if prev:
                    exp(b - 1, 7, 0, 7)
                    pT_split(b - 1, 6, 0)
                    pT_split(b - 1, 6, 1)
                if cur:
                    for n in range(3):
                        g_split(b, n)
                if prev:
                    pT_split(b - 1, 6, 2)
                    exp(b - 1, 7, 7, 10)
                if cur:
                    for n in range(3, 6):
                        g_split(b, n)
                    exp0(b, 0)
                if prev:
                    exp(b - 1, 7, 10, 16)
                if cur:
                    aT_split(b, 0)
                    exp0(b, 1)
                if prev:
                    for k in range(3):
                        pT_split(b - 1, 7, k)
                if cur:
                    aT_split(b, 1)
                    for i in range(TILES + X1T_LAG):
                        if i < TILES:
                            tanh(b, i)
                        if i >= X1T_LAG:
                            x1T_split(b, i - X1T_LAG)

            def batch(b, prev):
                head(b, prev, True)
                for s in range(TILES):
                    if s == 0:
                        for n in VO_IN_STEP[0]:
                            vo_split(b, n)
                        continue
                    if s == 1:
                        exp(b, 0, 0, HALVES[0][1])
                        for n in VO_IN_STEP[1]:
                            vo_split(b, n)
                        exp(b, 0, HALVES[1][0], HEADS)
                        continue
                    pT_split(b, s - 2, 0)
                    exp(b, s - 1, 0, 2)
                    pT_split(b, s - 2, 1)
                    exp(b, s - 1, 2, 5)
                    pT_split(b, s - 2, 2)
                    exp(b, s - 1, 5, HEADS)

            setup()
            act.wait_ge(su_dve, 2 * DC // 2 + PAIRS)
            act.wait_ge(pads_set, N_PADS)
            batch(0, False)
            with act.Fori(1, NB) as b:
                batch(b, True)
            head(NB, True, False)

        @block.vector
        def _(dve):
            v = nc.vector

            def setup():
                dve.wait_ge(ld_vec, 96)
                v.tensor_scalar(bk8[:, :], cols_sb[:, C_BK1:C_BK1 + PAIRS], SCALE, None, ALU.mult).then_inc(wsum_ready, 1)
                v.tensor_scalar(small[:, 0:1], small[:, 0:1], 0.5, None, ALU.mult).then_inc(vvs_chain, 1)
                v.tensor_tensor(bias_rows[:, 1, :], bias_rows[:, 1, :], bias_rows[:, 2, :], ALU.add).then_inc(vvs_chain, 1)
                dve.wait_ge(vvs_chain, 2)
                v.tensor_tensor(bias_rows[:, 1, :], bias_rows[:, 1, :], bias_rows[:, 3, :], ALU.add).then_inc(vvs_chain, 1)
                v.tensor_scalar(bias_rows[:, 0, :], bias_rows[:, 0, :], small[:, 0:1], None, ALU.mult).then_inc(vvs_chain, 1)
                dve.wait_ge(ld_w123, 48)
                v.tensor_tensor(wsum, w123[:, 0, :], w123[:, 1, :], ALU.add).then_inc(vvs_chain, 1)
                dve.wait_ge(vvs_chain, 5)
                dve.wait_ge(pads_set, N_PADS_EARLY)
                v.tensor_tensor(wsum, wsum, w123[:, 2, :], ALU.add).then_inc(wsum_ready, 1)
                for i, (what, n, who) in enumerate(SETUP):
                    if who != "dve":
                        continue
                    src = ps[i % 8][:, 0:AK]
                    dve.wait_ge(su_filled, i + 1)
                    if what == "vT0":
                        ins = v.tensor_scalar(vT0[:, n, :], src, cols_sb[:, C_BV0 + n:C_BV0 + n + 1], None, ALU.add)
                    elif what == "vh":
                        ins = v.tensor_scalar(vh_all[:, n, :], src, cols_sb[:, C_BV1 + n:C_BV1 + n + 1], None, ALU.add)
                    elif what == "rb0":
                        ins = v.tensor_copy(rb0[:, :], src)
                    else:
                        if n:
                            dve.wait_ge(vvs_step, 3 * n)
                        v.scalar_tensor_tensor(out=vvs_raw[0:KEYS, 0:D], in0=ps[i % 8][0:KEYS, 0:D], scalar=small[0:KEYS, 0:1],
                                               in1=bias_rows[0:KEYS, 0, :], op0=ALU.mult, op1=ALU.add).then_inc(su_dve, 1)
                        v.tensor_tensor(vvs_raw[0:KEYS, D:2 * D], ps[i % 8][0:KEYS, D:2 * D], bias_rows[0:KEYS, 1, :],
                                        ALU.add).then_inc(vvs_step, 1)
                        dve.wait_ge(vvs_step, 3 * n + 2)
                        v.tensor_tensor(vvs_lo[0:KEYS, n * BANK:(n + 1) * BANK], vvs_raw[0:KEYS, :],
                                        vvs_hi[0:KEYS, n * BANK:(n + 1) * BANK], ALU.subtract).then_inc(vvs_step, 1)
                        continue
                    ins.then_inc(su_dve, 1)

            def blk_v_copy(b, prev):
                if prev:
                    dve.wait_ge(vo_filled, b * VO_FILLS)
                view = blk_v[:, P:].rearrange("p (r n) -> p r n", r=PAIRS)
                v.tensor_copy(view[0:DK, :, 0:KEYS], vh_all[0:DK, :, bass.ds(b * KEYS, KEYS)])
                v.tensor_copy(view[DK:P, :, KEYS:PW], vh_all[DK:P, :, bass.ds(b * KEYS, KEYS)]).then_inc(blk_v_ready, 1)

            def energy(b, g):
                e = attn[:, g * GROUP * P:(g + 1) * GROUP * P].rearrange("p (i n) -> p i n", i=GROUP)[:, :, 0:KEYS]
                dve.wait_ge(energy_filled, b * GROUPS + g + 1)
                v.tensor_tensor(e, L0_BANK[g][:, :].rearrange("p (i n) -> p i n", i=GROUP)[:, :, 0:KEYS],
                                rb0[:, bass.ds(b * KEYS, KEYS)].unsqueeze(1).broadcast_to([P, GROUP, KEYS]), ALU.add).then_inc(e_biased, 1)
                dve.wait_ge(e_biased, b * GROUPS + g + 1)
                v.tensor_reduce(negmax0[:, g * GROUP:(g + 1) * GROUP], e, AX.X, ALU.max, negate=True).then_inc(negmax0_ready, 1)

            def rsum0_of(b, g):
                dve.wait_ge(exp0_done, b * GROUPS + g + 1)
                v.reciprocal(rsum0[:, g * GROUP:(g + 1) * GROUP], sums0[:, g * GROUP:(g + 1) * GROUP]).then_inc(rsum0_ready, 1)

            def g_split(b, n):
                c, k = n // 3, n % 3
                a, e = SCORE_COLS[k]
                dve.wait_ge(g_hi_ready, b * 6 + n + 1)
                v.tensor_tensor(g_lo[:, c, a:e], S_BANK[k][:, 0:e - a], g_hi[:, c, a:e], ALU.subtract).then_inc(g_lo_ready, 1)

            def rb_copy(b, k, prev):
                a, e = SCORE_COLS[k]
                if k == 0 and prev:
                    dve.wait_ge(f_biased, b * TILES)
                dve.wait_ge(rb_filled, 3 * b + k + 1)
                v.tensor_scalar(rb1[:, a:e], S_BANK[k][:, 0:e - a], 0.5, None, ALU.mult).then_inc(rb1_ready, 1)

            def aT_split(b, g):
                dve.wait_ge(aT_hi_ready, b * GROUPS + g + 1)
                sl = slice(g * GROUP, (g + 1) * GROUP)
                v.tensor_tensor(aT_lo[:, sl, :].rearrange("p i n -> p (i n)"), L0_BANK[g][:, :],
                                aT_hi[:, sl, :].rearrange("p i n -> p (i n)"), ALU.subtract).then_inc(aT_lo_ready, 1)

            def gate(b, i, prev):
                dve.wait_ge(tanh_ready, b * TILES + i + 1)
                if i >= 2 or prev:
                    dve.wait_ge(x1_ready, b * TILES + i - 1)
                v.scalar_tensor_tensor(out=o_sb[:, i % 2, :], in0=th[:, i % 2, :], scalar=1.0, in1=GATE_BANK[i % NG][:, 0:D],
                                       op0=ALU.add, op1=ALU.mult).then_inc(gated, 1)

            def x1T_split(b, i):
                dve.wait_ge(x1T_hi_ready, b * TILES + i + 1)
                v.tensor_tensor(x1T_lo[:, i, :], X1T_BANK[i % NX][:, 0:D], x1T_hi[:, i, :], ALU.subtract).then_inc(x1T_lo_ready, 1)

            def vo_split(b, n):
                dve.wait_ge(vo_hi_ready, b * VO_FILLS + n + 1)
                v.tensor_tensor(vo_lo[:, 2 * n:2 * n + 2, :].rearrange("p c n -> p (c n)"), T_BANK[n % 2][:, :],
                                vo_hi[:, 2 * n:2 * n + 2, :].rearrange("p c n -> p (c n)"), ALU.subtract).then_inc(vo_lo_ready, 1)

            def s_bias(b, s, k):
                a, e = SCORE_COLS[k]
                if k == 0:
                    dve.wait_ge(f_biased, b * TILES + s + 1)
                dve.wait_ge(scores_filled, 3 * (b * TILES + s) + k + 1)
                v.scalar_tensor_tensor(out=f_slot(s, a, e), in0=f_slot(s, a, e), scalar=2.0, in1=S_BANK[k][:, 0:e - a],
                                       op0=ALU.mult, op1=ALU.add).then_inc(s_biased, 1)

            def s_max(b, s):
                dve.wait_ge(s_biased, 3 * (b * TILES + s + 1))
                v.tensor_reduce(negmax[:, s % 2, :], f_slot(s).rearrange("p (h n) -> p h n", h=HEADS), AX.X, ALU.max,
                                negate=True).then_inc(negmax_ready, 1)

            def recip(b, s, half):
                h0, h1 = HALVES[half]
                dve.wait_ge(exp_done, 2 * (b * TILES + s) + half + 1)
                v.reciprocal(rsum[:, s % 2, h0:h1], sums[:, s % 2, h0:h1]).then_inc(rsum_ready, 1)

            def pT_split(b, s, k):
                c0, c1 = PT_FILLS[k]
                dve.wait_ge(pT_hi_ready, 3 * (b * TILES + s) + k + 1)
                v.tensor_tensor(pt_lo[:, c0:c1, :].rearrange("p c n -> p (c n)"), T_BANK[PT_BANK[k]][:, 0:(c1 - c0) * P],
                                pt_hi[:, c0:c1, :].rearrange("p c n -> p (c n)"), ALU.subtract).then_inc(pT_lo_ready, 1)

            def ln_stats(b, s, may_be_first):
                t = b * TILES + s
                if not (may_be_first and s < YSLOTS):
                    dve.wait_ge(out_stored[s % YSLOTS], 16 * (TILES // YSLOTS) * b + 16 * (s // YSLOTS))
                dve.wait_ge(out_filled, t + 1)
                yt = y[:, s % YSLOTS, :]
                v.tensor_tensor(yt, O_BANK[:, 0:D], xrow[:, s * D:(s + 1) * D], ALU.add).then_inc(y_summed, 1)
                dve.wait_ge(y_summed, t + 1)
                v.bn_stats(stats[:, :], yt).then_inc(y_stats, 1)
                dve.wait_ge(ld_vec, 96)
                dve.wait_ge(y_stats, t + 1)
                v.bn_aggr(meanvar[:, s % YSLOTS, :], stats[:, :]).then_inc(y_meanvar, 1)
                dve.wait_ge(y_meanvar, t + 1)
                v.tensor_scalar(var_eps[:, s % YSLOTS:s % YSLOTS + 1], meanvar[:, s % YSLOTS, 1:2], EPS, None, ALU.add).then_inc(var_ready, 1)

            def ln_norm(b, s):
                yt = y[:, s % YSLOTS, :]
                dve.wait_ge(rstd_ready, b * TILES + s + 1)
                v.tensor_scalar(yt, yt, meanvar[:, s % YSLOTS, 0:1], rstd[:, s % YSLOTS:s % YSLOTS + 1],
                                ALU.subtract, ALU.mult).then_inc(y_normed, 1)

            def head(b, prev, cur):
                if cur:
                    blk_v_copy(b, prev)
                    energy(b, 0)
                    energy(b, 1)
                if prev:
                    pT_split(b - 1, 6, 0)
                    pT_split(b - 1, 6, 1)
                    ln_norm(b - 1, 5)
                if cur:
                    for n in range(3):
                        g_split(b, n)
                if prev:
                    pT_split(b - 1, 6, 2)
                    recip(b - 1, 7, 0)
                if cur:
                    for n in range(3, 6):
                        g_split(b, n)
                    rsum0_of(b, 0)
                if prev:
                    ln_stats(b - 1, 6, False)
                    recip(b - 1, 7, 1)
                if cur:
                    aT_split(b, 0)
                    rsum0_of(b, 1)
                if prev:
                    ln_norm(b - 1, 6)
                    pT_split(b - 1, 7, 0)
                    pT_split(b - 1, 7, 1)
                if cur:
                    rb_copy(b, 0, prev)
                    rb_copy(b, 1, prev)
                if prev:
                    pT_split(b - 1, 7, 2)
                if cur:
                    rb_copy(b, 2, prev)
                    aT_split(b, 1)
                if prev:
                    ln_stats(b - 1, 7, False)
                if cur:
                    for i in range(TILES + X1T_LAG):
                        if i < TILES:
                            gate(b, i, prev)
                        if i >= X1T_LAG:
                            x1T_split(b, i - X1T_LAG)
                        if i == 1 and prev:
                            ln_norm(b - 1, 7)
                elif prev:
                    ln_norm(b - 1, 7)

            def batch(b, prev):
                head(b, prev, True)
                for s in range(TILES):
                    if s < 2:
                        for k in range(3):
                            s_bias(b, s, k)
                        s_max(b, s)
                        if s:
                            recip(b, 0, 0)
                        for n in VO_IN_STEP[s]:
                            vo_split(b, n)
                        if s:
                            recip(b, 0, 1)
                        continue
                    pT_split(b, s - 2, 0)
                    s_bias(b, s, 0)
                    pT_split(b, s - 2, 1)
                    if s > 2:
                        ln_norm(b, s - 3)
                    s_bias(b, s, 1)
                    pT_split(b, s - 2, 2)
                    recip(b, s - 1, 0)
                    s_bias(b, s, 2)
                    s_max(b, s)
                    recip(b, s - 1, 1)
                    ln_stats(b, s - 2, not prev)

            setup()
            dve.wait_ge(su_filled, N_SETUP)
            dve.wait_ge(su_act, evacuated(HEAD_WEIGHTS_USED + DC - 1)[1])
            dve.wait_ge(pads_set, N_PADS)
            batch(0, False)
            with dve.Fori(1, NB) as b:
                batch(b, True)
            head(NB, True, False)

        @block.gpsimd
        def _(pool):
            g_ = nc.gpsimd

            def f_bias(b, s):
                pool.wait_ge(f_loaded[s % SLOTS], 16 * ((TILES // SLOTS) * b + s // SLOTS + 1))
                if s == 0:
                    pool.wait_ge(rb1_ready, 3 * (b + 1))
                g_.tensor_tensor(f_slot(s), f_slot(s), rb1[:, :], ALU.add).then_inc(f_biased, 1)

            def normalise(b, s, half):
                h0, h1 = HALVES[half]
                pool.wait_ge(rsum_ready, 2 * (b * TILES + s) + half + 1)
                p = f_slot(s, h0 * KEYS, h1 * KEYS).rearrange("p (h n) -> p h n", n=KEYS)
                g_.tensor_tensor(p, p, rsum[:, s % 2, h0:h1].unsqueeze(2).broadcast_to([P, h1 - h0, KEYS]), ALU.mult).then_inc(probs_ready, 1)

            def normalise0(b, g):
                pool.wait_ge(rsum0_ready, b * GROUPS + g + 1)
                e = attn[:, g * GROUP * P:(g + 1) * GROUP * P].rearrange("p (i n) -> p i n", i=GROUP)[:, :, 0:KEYS]
                g_.tensor_tensor(e, e, rsum0[:, g * GROUP:(g + 1) * GROUP].unsqueeze(2).broadcast_to([P, GROUP, KEYS]),
                                 ALU.mult).then_inc(attn_ready, 1)

            def x1(b, i):
                if i % GROUP == 0:
                    pool.wait_ge(x_loaded[i // GROUP], 16 * (b + 1))
                pool.wait_ge(gated, b * TILES + i + 1)
                xt = xrow[:, i * D:(i + 1) * D]
                g_.tensor_tensor(xt, xt, o_sb[:, i % 2, :], ALU.add).then_inc(x1_ready, 1)

            def rstd_of(b, s):
                pool.wait_ge(var_ready, b * TILES + s + 1)
                j = s % YSLOTS
                g_.tensor_tensor(rstd[:, j:j + 1], var_eps[:, j:j + 1], small[:, 1:2], ALU.pow).then_inc(rstd_ready, 1)

            def ln_affine(b, s):
                yt = y[:, s % YSLOTS, :]
                pool.wait_ge(y_normed, b * TILES + s + 1)
                g_.tensor_tensor(yt, yt, ln_gb[:, 0, :], ALU.mult).then_inc(y_scaled, 1)
                pool.wait_ge(y_scaled, b * TILES + s + 1)
                g_.tensor_tensor(yt, yt, ln_gb[:, 1, :], ALU.add).then_inc(y_final, 1)

            def head(b, prev, cur):
                if prev:
                    rstd_of(b - 1, 5)
                    ln_affine(b - 1, 5)
                    normalise(b - 1, 7, 0)
                if cur:
                    normalise0(b, 0)
                if prev:
                    rstd_of(b - 1, 6)
                    normalise(b - 1, 7, 1)
                if cur:
                    normalise0(b, 1)
                if prev:
                    ln_affine(b - 1, 6)
                    rstd_of(b - 1, 7)
                if cur:
                    for i in range(TILES):
                        x1(b, i)
                        if i == 1 and prev:
                            ln_affine(b - 1, 7)
                        if i == 3:
                            f_bias(b, 0)
                else:
                    ln_affine(b - 1, 7)

            def batch(b, prev):
                head(b, prev, True)
                for s in range(TILES):
                    if s > 2:
                        rstd_of(b, s - 3)
                    if s + 1 < TILES:
                        f_bias(b, s + 1)
                    if s > 2:
                        ln_affine(b, s - 3)
                    if s:
                        normalise(b, s - 1, 0)
                        normalise(b, s - 1, 1)

            g_.memset(small[:, 1:2], -0.5).then_inc(pads_set, 1)
            g_.memset(sel_h0[:, :], 0.0).then_inc(pool_chain, 1)
            pool.wait_ge(pool_chain, 1)
            g_.memset(sel_h0[:, 0:KEYS], 1.0).then_inc(pads_set, 1)
            g_.memset(vvs_hi[:, :].bitcast(F32), 0.0).then_inc(pads_set, 1)
            g_.memset(vvs_lo[:, :].bitcast(F32), 0.0).then_inc(pads_set, 1)
            g_.memset(m_all[:, :, AK:], 0.0).then_inc(pads_set, 1)
            pool.wait_ge(su_filled, HEAD_WEIGHTS_USED)
            g_.memset(fs[:, :].rearrange("p (s n) -> p s n", s=SLOTS)[:, :, HK:], 0.0).then_inc(pads_set, 1)
            pool.wait_ge(su_filled, N_SETUP)
            pool.wait_ge(vvs_step, 3 * NB)
            g_.memset(attn[:, :].rearrange("p (i n) -> p i n", i=TILES)[:, :, KEYS:], 0.0).then_inc(pads_set, 1)
            g_.memset(blk_k[:, :], 0.0).then_inc(pads_set, 1)
            g_.memset(blk_v[:, :], 0.0).then_inc(pads_set, 1)
            batch(0, False)
            with pool.Fori(1, NB) as b:
                batch(b, True)
            head(NB, True, False)


_OUT = (NB, SEQ, D)


def kernel(**inputs):
    import numpy as np
    import concourse.bacc as bacc
    from concourse.bass_utils import run_bass_kernel_spmd

    a = {k: np.asarray(v) for k, v in inputs.items()}
    l0 = {k[9:]: v for k, v in a.items() if k.startswith("L0_xattn_")}
    l1 = {k[9:]: v for k, v in a.items() if k.startswith("L1_xattn_")}
    x = a["x"].reshape(NB * SEQ, D)
    chunks = [v.reshape(-1, P).T for v in (l0["bk"], l0["bv"], l0["bq"], l1["bq"], l1["bk"], l1["bv"])]
    arrays = {
        "x": x, "xT": x.T, "cT": a["ctx_1024"].reshape(AK, D).T,
        "fside": a["fside_Bx16xSxS2_0"].transpose(0, 2, 1, 3).reshape(NB * SEQ, HK),
        "wq0": l0["Wq"], "wk0T": l0["Wk"].T, "wv0T": l0["Wv"].T,
        "w1T": l0["W1"].T, "w2T": l0["W2"].T, "w3T": l0["W3"].T,
        "wqT": l1["wq"].T, "wk": l1["wk"], "wv": l1["wv"], "wo": l1["wo"],
        "cols": np.concatenate(chunks, axis=1),
        "rows": np.stack([l0["bv"], l0["b1"], l0["b2"], l0["b3"], l1["ln_g"], l1["ln_b"]]),
        "bo": l1["bo"].reshape(1, D), "gamma": l0["gamma"].reshape(1), "ident_in": np.eye(P, dtype=np.float32),
    }
    arrays = {f"in_{k}": np.ascontiguousarray(v) for k, v in arrays.items()}
    nc = bacc.Bacc("TRN2", target_bir_lowering=False, num_devices=1)
    args = [nc.dram_tensor(k, v.shape, mybir.dt.from_np(v.dtype), kind="ExternalInput").ap() for k, v in arrays.items()]
    args.append(nc.dram_tensor("out_0", (NB * SEQ, D), F32, kind="ExternalOutput").ap())
    build(nc, *args)
    r = run_bass_kernel_spmd(nc, [arrays], core_ids=[0])
    return r.results[0]["out_0"].reshape(_OUT)
```

```python
from contextlib import ExitStack

import concourse.bass as bass
from concourse import mybir

F32 = mybir.dt.float32
F32R = mybir.dt.float32r
ALU = mybir.AluOpType
ACT = mybir.ActivationFunctionType
AX = mybir.AxisListType

P = 128
NB, SEQ, D = 4, 1024, 256
KEYS, HEADS, DK = 77, 16, 64
DC = D // P
TILES = SEQ // P
GROUP = 4
GROUPS = TILES // GROUP
X_PIECES = [(0, 4), (4, 7), (7, 8)]
PAIRS = HEADS // 2
HK = HEADS * KEYS
HKP = -(-HK // P) * P
CH = HKP // P
PW = 2 * KEYS
AK = NB * KEYS
BANK = 512
SCORE_PAIRS = [(0, 3), (3, 6), (6, 8)]
SCORE_COLS = [(a * PW, b * PW) for a, b in SCORE_PAIRS]
PT_FILLS = [(0, 4), (4, 8), (8, 10)]
PT_BANK = [0, 1, 0]
HALVES = [(0, HEADS // 2), (HEADS // 2, HEADS)]
W_HALVES = [(h0 * DK, h1 * DK) for h0, h1 in HALVES]
SLOTS = 4
YSLOTS = 4
VSTRIDE = P + PW
VWIDTH = P + PAIRS * VSTRIDE
SCALE = DK ** -0.5
EPS = 1e-6
VO_FILLS = CH // 2
WARM_UPS = 8
L0_EARLY = 4
X1T_AFTER = {4: [0], 5: [1, 2], 6: [3], 7: [4, 5]}
X1T_LATE = [6, 7]
EXP7_SPLIT = [8, 10, 11, 12]
assert SCALE == 0.125 and CH == PT_FILLS[-1][1]
C_BK0, C_BV0, C_BQ0, C_BQ1, C_BK1, C_BV1 = 0, 2, 4, 6, 14, 22
NCOLS = 30
R_B1, R_B2, R_B3, R_LNG, R_LNB = range(5)


def build(nc, x, xT, cT, fside, wq0, wk0T, wv0T, w1T, w2T, w3T, wqT, wk, wv, wo, cols, rows, bo, gamma, ident_in, out, rb_dram):
    x_v = x.rearrange("(b t p) d -> p b t d", b=NB, t=TILES)
    xT_v = xT.rearrange("(c p) n -> p c n", p=P)
    f_v = fside.rearrange("(t p) n -> p t n", p=P)
    out_v = out.rearrange("(t p) n -> p t n", p=P)

    with ExitStack() as ctx:
        def sb(name, shape, dt=F32):
            return ctx.enter_context(nc.sbuf_tensor(name, shape, dt))

        def sem(name):
            return ctx.enter_context(nc.semaphore(name))

        wqT_sb = sb("wqT_sb", [P, PAIRS, D])
        wo_sb = sb("wo_sb", [P, PAIRS, D])
        kh_all = sb("kh_all", [P, PAIRS, AK])
        vh_all = sb("vh_all", [P, PAIRS, AK])
        bq_blk = sb("bq_blk", [P, PAIRS * HEADS])
        rb_all = sb("rb_all", [HEADS, AK])
        m_all = sb("m_all", [P, DC, (NB - 1) * KEYS + P])
        rb0 = sb("rb0", [P, AK])
        vvs_hi = sb("vvs_hi", [P, NB * BANK], F32R)
        vvs_lo = sb("vvs_lo", [P, NB * BANK], F32R)
        ln_gb = sb("ln_gb", [P, 2, D])
        ident = sb("ident", [P, P])
        cols_sb = sb("cols_sb", [P, NCOLS])
        small = sb("small", [P, 8])
        bk8 = sb("bk8", [P, PAIRS])
        bo_sb = sb("bo_sb", [1, D])
        sel_h0 = sb("sel_h0", [1, P])
        blk_k = sb("blk_k", [P, PAIRS * PW])
        blk_v = sb("blk_v", [P, VWIDTH])
        g_hi = sb("g_hi", [P, DC, HK], F32R)
        g_lo = sb("g_lo", [P, DC, HK], F32R)
        vo_hi = sb("vo_hi", [P, CH, D], F32R)
        vo_lo = sb("vo_lo", [P, CH, D], F32R)
        rb1 = sb("rb1", [P, HK])
        fs = sb("fs", [P, SLOTS * HKP])
        pt_hi = sb("pt_hi", [P, CH, P], F32R)
        pt_lo = sb("pt_lo", [P, CH, P], F32R)
        x1T_hi = sb("x1T_hi", [P, TILES, D], F32R)
        x1T_lo = sb("x1T_lo", [P, TILES, D], F32R)
        xrow = sb("xrow", [P, TILES * D])
        xT_sb = sb("xT_sb", [P, DC, SEQ])
        attn = sb("attn", [P, TILES * P])
        aT_hi = sb("aT_hi", [P, TILES, P], F32R)
        aT_lo = sb("aT_lo", [P, TILES, P], F32R)
        work = sb("work", [P, (YSLOTS + 4) * D])
        y = work[:, 0:YSLOTS * D].rearrange("p (s d) -> p s d", s=YSLOTS)
        th = work[:, YSLOTS * D:(YSLOTS + 2) * D].rearrange("p (s d) -> p s d", s=2)
        o_sb = work[:, (YSLOTS + 2) * D:(YSLOTS + 4) * D].rearrange("p (s d) -> p s d", s=2)
        negmax = sb("negmax", [P, 2, HEADS])
        sums = sb("sums", [P, 2, HEADS])
        rsum = sb("rsum", [P, 2, HEADS])
        negmax0 = sb("negmax0", [P, TILES])
        sums0 = sb("sums0", [P, TILES])
        rsum0 = sb("rsum0", [P, TILES])
        stats = sb("stats", [P, 6])
        meanvar = sb("meanvar", [P, YSLOTS, 2])
        var_eps = sb("var_eps", [P, YSLOTS])
        rstd = sb("rstd", [P, YSLOTS])

        fs_slots = fs[:, :].rearrange("p (s n) -> p s n", s=SLOTS)
        wk_sb = fs_slots[:, 0:DC, 0:HEADS * DK]
        wv_sb = fs_slots[:, DC:2 * DC, 0:HEADS * DK]
        w123 = xrow[:, 0:3 * DC * D].rearrange("p (w n) -> p w n", w=3)
        wsum = attn[:, 0:DC * D]
        warm = attn[:, DC * D:DC * D + P]
        wk_hi, wk_lo = (t[:, :, 0:HEADS * DK] for t in (g_hi, g_lo))
        wv_hi, wv_lo = (t[:, 0:DC * HEADS * DK // D, :].rearrange("p (c k) n -> p c (k n)", c=DC) for t in (vo_hi, vo_lo))
        cT_hi, cT_lo = (t[:, :, :].rearrange("p i n -> p (i n)")[:, 0:DC * AK].rearrange("p (c n) -> p c n", c=DC) for t in (aT_hi, aT_lo))
        wk0_sb = work[:, 0:DC * D].rearrange("p (c n) -> p c n", c=DC)
        wv0_sb = work[:, DC * D:2 * DC * D].rearrange("p (c n) -> p c n", c=DC)
        wq0_sb = work[:, 2 * DC * D:3 * DC * D].rearrange("p (c n) -> p c n", c=DC)
        vvs_raw = [work[0:KEYS, 3 * DC * D:3 * DC * D + BANK], work[0:KEYS, 0:BANK]]
        kT0 = blk_v[:, 0:DC * AK].rearrange("p (c n) -> p c n", c=DC)
        vT0 = blk_v[:, DC * AK:2 * DC * AK].rearrange("p (c n) -> p c n", c=DC)
        cT_sb = rb1[:, 0:DC * AK].rearrange("p (c n) -> p c n", c=DC)
        bias_rows = blk_k[:, 0:3 * D].rearrange("p (r d) -> p r d", r=3)
        bq0_rep = rb1[:, DC * AK:DC * AK + DC * P].rearrange("p (c n) -> p c n", c=DC)

        ps = [ctx.enter_context(nc.psum_tensor(f"bank{i}", [P, BANK], F32)) for i in range(8)]
        S_BANK, T_BANK, O_BANK, E_BANK, X_BANK = ps[0:3], ps[3:5], ps[5], ps[6], ps[7]
        L0_BANK = [E_BANK, X_BANK]
        VO_BANK = [E_BANK, X_BANK]
        GATE_BANK = [E_BANK, X_BANK, S_BANK[1], S_BANK[2]]
        X1T_BANK = [T_BANK[1], O_BANK, S_BANK[0]]
        NG, NX = len(GATE_BANK), len(X1T_BANK)
        X1T_IN_S0 = max(i for i in range(TILES) if i % NX == 2)

        ld_ctx, ld_wk0, ld_wv0, ld_wq0, ld_wk, ld_wv = (sem(f"ld_{n}") for n in ("ctx", "wk0", "wv0", "wq0", "wk", "wv"))
        ld_w123, ld_cols, ld_ident, ld_vec, ld_w1 = (sem(f"ld_{n}") for n in ("w123", "cols", "ident", "vec", "w1"))
        f_loaded = [sem(f"f_loaded{i}") for i in range(SLOTS)]
        xT_loaded = sem("xT_loaded")
        x_loaded = [sem(f"x_loaded{g}") for g in range(len(X_PIECES))]
        out_stored = [sem(f"out_stored{i}") for i in range(YSLOTS)]
        consts_set, wsum_ready, su_filled, su_act, su_dve = (sem(n) for n in ("consts_set", "wsum_ready", "su_filled", "su_act", "su_dve"))
        cT_hi_ready, cT_lo_ready, w_hi_ready, w_lo_ready = (sem(n) for n in ("cT_hi_ready", "cT_lo_ready", "w_hi_ready", "w_lo_ready"))
        vvs_hi_ready, vvs_lo_ready, pads_set, bq_ready, warm_ready = (sem(n) for n in ("vvs_hi_ready", "vvs_lo_ready", "pads_set", "bq_ready", "warm_ready"))
        vvs_chain, pool_chain, rb_stored, rb_loaded = (sem(n) for n in ("vvs_chain", "pool_chain", "rb_stored", "rb_loaded"))
        energy_filled, g_filled, attnT_filled = (sem(n) for n in ("energy_filled", "g_filled", "attnT_filled"))
        l0_filled, x1T_filled, vo_filled = (sem(n) for n in ("l0_filled", "x1T_filled", "vo_filled"))
        scores_filled, pT_filled, out_filled = (sem(n) for n in ("scores_filled", "pT_filled", "out_filled"))
        blk_k_ready, g_hi_ready, exp0_done, aT_hi_ready = (sem(n) for n in ("blk_k_ready", "g_hi_ready", "exp0_done", "aT_hi_ready"))
        tanh_ready, x1T_hi_ready, vo_hi_ready, pT_hi_ready, exp_done = (sem(n) for n in ("tanh_ready", "x1T_hi_ready", "vo_hi_ready", "pT_hi_ready", "exp_done"))
        blk_v_ready, e_biased, negmax0_ready, rsum0_ready, g_lo_ready = (sem(n) for n in ("blk_v_ready", "e_biased", "negmax0_ready", "rsum0_ready", "g_lo_ready"))
        aT_lo_ready, gated, x1T_lo_ready, vo_lo_ready = (sem(n) for n in ("aT_lo_ready", "gated", "x1T_lo_ready", "vo_lo_ready"))
        s_biased, negmax_ready, rsum_ready, pT_lo_ready = (sem(n) for n in ("s_biased", "negmax_ready", "rsum_ready", "pT_lo_ready"))
        y_summed, y_stats, y_meanvar, var_ready, y_normed = (sem(n) for n in ("y_summed", "y_stats", "y_meanvar", "var_ready", "y_normed"))
        attn_ready, x1_ready, f_biased, probs_ready = (sem(n) for n in ("attn_ready", "x1_ready", "f_biased", "probs_ready"))
        rstd_ready, y_scaled, y_final = (sem(n) for n in ("rstd_ready", "y_scaled", "y_final"))

        def f_slot(s, a=0, b=HK):
            return fs[:, (s % SLOTS) * HKP + a:(s % SLOTS) * HKP + b]

        SETUP = ([("kT0", i, "act") for i in range(DC)] + [("vT0", i, "dve") for i in range(DC)]
                 + [("m", i, "act") for i in range(DC)] + [("rb0", 0, "dve")] + [("vvs", b, "dve") for b in range(NB)]
                 + [("kh", j, "act") for j in range(PAIRS)] 
                 + [("vh", j, "dve") for j in range(2)] + [("rb1", 0, "dve")] + [("vh", j, "dve") for j in range(2, PAIRS)])
        N_SETUP = len(SETUP)
        FILL_OF = {(what, n): i for i, (what, n, _) in enumerate(SETUP)}
        VVS_DONE, KH_DONE = FILL_OF["vvs", NB - 1] + 1, FILL_OF["kh", PAIRS - 1] + 1
        N_PADS_EARLY, N_PADS = 7, 10

        def evacuated(i):
            who = SETUP[i][2]
            return (su_act if who == "act" else su_dve), sum(w == who for _, _, w in SETUP[:i + 1])

        block = ctx.enter_context(nc.Block())

        @block.sync
        def _(sp):
            def load_xT(b):
                sp.dma_start(xT_sb[:, :, :], xT_v[:, :, bass.ds(b * SEQ, SEQ)]).then_inc(xT_loaded, 16)

            def load_x(b, g):
                t0, t1 = X_PIECES[g]
                sp.dma_start(xrow[:, t0 * D:t1 * D].rearrange("p (i d) -> p i d", i=t1 - t0),
                             x_v[:, bass.ds(b, 1), t0:t1, :].rearrange("p b i d -> p (b i) d")).then_inc(x_loaded[g], 16)

            def load_f(b, s):
                sp.dma_start(f_slot(s), f_v[:, bass.ds(b * TILES + s, 1), :].rearrange("p t n -> p (t n)")).then_inc(f_loaded[s % SLOTS], 16)

            def load_rb(b):
                sp.dma_start(rb1[:, :], rb_dram[bass.ds(b, 1), :].rearrange("b n -> (b n)").partition_broadcast(P)).then_inc(rb_loaded, 16)

            def store(b, s):
                sp.wait_ge(y_final, b * TILES + s + 1)
                sp.dma_start(out_v[:, bass.ds(b * TILES + s, 1), :].rearrange("p t n -> p (t n)"),
                             y[:, s % YSLOTS, :]).then_inc(out_stored[s % YSLOTS], 16)

            def batch(b, first, last):
                if not first:
                    store(b - 1, 5)
                    sp.wait_ge(y_summed, b * TILES - 1)
                    load_x(b, 1)
                    store(b - 1, 6)
                    sp.wait_ge(y_summed, b * TILES)
                    load_x(b, 2)
                for s in range(TILES):
                    if s >= 2:
                        sp.wait_ge(pT_filled, 3 * (b * TILES + s - 1))
                        if s + 2 < TILES:
                            load_f(b, s + 2)
                        elif not last:
                            load_f(b + 1, s + 2 - TILES)
                    elif s + 2 < TILES:
                        if not first:
                            sp.wait_ge(pT_filled, 3 * (b * TILES + s - 1))
                        load_f(b, s + 2)
                    if s == 1 and not first:
                        store(b - 1, 7)
                    if s == 0 and not last:
                        sp.wait_ge(energy_filled, GROUPS * (b + 1))
                        load_xT(b + 1)
                    if s >= 3:
                        store(b, s - 3)
                    if s == 7 and not last:
                        sp.wait_ge(f_biased, (b + 1) * TILES)
                        load_rb(b + 1)
                    if s == 6 and not last:
                        sp.wait_ge(y_summed, b * TILES + 4)
                        load_x(b + 1, 0)

            sp.dma_start(cT_sb, cT.rearrange("(c p) n -> p c n", p=P)).then_inc(ld_ctx, 16)
            sp.dma_start(wk0_sb, wk0T.rearrange("(c p) n -> p c n", p=P)).then_inc(ld_wk0, 16)
            sp.dma_start(wv0_sb, wv0T.rearrange("(c p) n -> p c n", p=P)).then_inc(ld_wv0, 16)
            sp.dma_start(wq0_sb, wq0.rearrange("(c p) n -> p c n", p=P)).then_inc(ld_wq0, 16)
            for i, w in enumerate((w1T, w2T, w3T)):
                sp.dma_start(w123[:, i, :].rearrange("p (c n) -> p c n", c=DC), w.rearrange("(c p) n -> p c n", p=P)).then_inc(ld_w123, 16)
            sp.dma_start(wk_sb, wk.rearrange("(c p) n -> p c n", p=P)).then_inc(ld_wk, 16)
            sp.dma_start(wv_sb, wv.rearrange("(c p) n -> p c n", p=P)).then_inc(ld_wv, 16)
            load_xT(0)
            sp.dma_start(wqT_sb[:, :, :], wqT.rearrange("(c p) n -> p c n", p=P)).then_inc(ld_w1, 16)
            sp.dma_start(wo_sb[:, :, :], wo.rearrange("(c p) n -> p c n", p=P)).then_inc(ld_w1, 16)
            sp.wait_ge(wsum_ready, 2)
            load_x(0, 0)
            load_x(0, 1)
            load_x(0, 2)
            sp.wait_ge(su_filled, KH_DONE)
            load_f(0, 0)
            load_f(0, 1)
            sp.wait_ge(*evacuated(FILL_OF["rb1", 0]))
            sp.dma_start(rb_dram.rearrange("b (h n) -> h b n", h=HEADS), rb_all[:, :].rearrange("h (b n) -> h b n", b=NB)).then_inc(rb_stored, 16)
            sp.wait_ge(rb_stored, 16)
            sp.wait_ge(su_filled, N_SETUP)
            load_rb(0)
            batch(0, True, False)
            with sp.Fori(1, NB - 1) as b:
                batch(b, False, False)
            batch(NB - 1, False, True)
            for s in (5, 6, 7):
                store(NB - 1, s)
            for i in range(YSLOTS):
                sp.wait_ge(out_stored[i], 16 * NB * TILES // YSLOTS)

        @block.tensor
        def _(pe):
            mm = nc.tensor.matmul

            def three_pass(dst, a_hi, a_lo, b_hi, b_lo, start, stop):
                mm(dst, a_hi, b_hi, start=start, stop=False)
                mm(dst, a_hi, b_lo, start=False, stop=False)
                return mm(dst, a_lo, b_hi, start=False, stop=stop)

            def setup():
                pe.wait_ge(warm_ready, 1)
                for _ in range(WARM_UPS):
                    mm(ps[7][:, 0:P], warm, warm, start=True, stop=True)
                pe.wait_ge(ld_ctx, 16)
                loads = {"kT0": (ld_wk0, 16), "vT0": (ld_wv0, 16), "m": (ld_wq0, 16)}
                for i, (what, n, _) in enumerate(SETUP):
                    if i >= 8:
                        pe.wait_ge(*evacuated(i - 8))
                    dst = ps[i % 8]
                    if n == 0 and what in loads:
                        pe.wait_ge(*loads[what])
                    if what in ("kh", "vh"):
                        pe.wait_ge(w_lo_ready, (1 if what == "kh" else 3) + n // (PAIRS // 2))
                    if what == "kh" and n == 0:
                        pe.wait_ge(cT_lo_ready, 1)
                    if what == "m" and n == 0:
                        pe.wait_ge(*evacuated(FILL_OF["kT0", DC - 1]))
                    if what == "rb0":
                        pe.wait_ge(consts_set, 1)
                    if what == "rb1":
                        pe.wait_ge(bq_ready, 1)
                        pe.wait_ge(*evacuated(FILL_OF["kh", PAIRS - 1]))
                        for pr in range(PAIRS):
                            ins = mm(dst[0:HEADS, 0:AK], bq_blk[:, pr * HEADS:(pr + 1) * HEADS], kh_all[:, pr, :], start=pr == 0, stop=pr == PAIRS - 1)
                        ins.then_inc(su_filled, 1)
                        continue
                    if what == "vvs" and n == 0:
                        pe.wait_ge(ld_ident, 16)
                        pe.wait_ge(*evacuated(FILL_OF["vT0", DC - 1]))
                        pe.wait_ge(wsum_ready, 2)
                    for c in range(DC):
                        first, last = c == 0, c == DC - 1
                        if what == "kT0":
                            ins = mm(dst[:, 0:AK], wk0_sb[:, c, n * P:(n + 1) * P], cT_sb[:, c, :], start=first, stop=last)
                        elif what == "vT0":
                            ins = mm(dst[:, 0:AK], wv0_sb[:, c, n * P:(n + 1) * P], cT_sb[:, c, :], start=first, stop=last)
                        elif what == "kh":
                            ins = three_pass(dst[:, 0:AK], wk_hi[:, c, n * P:(n + 1) * P], wk_lo[:, c, n * P:(n + 1) * P],
                                             cT_hi[:, c, :], cT_lo[:, c, :], first, last)
                        elif what == "vh":
                            ins = three_pass(dst[:, 0:AK], wv_hi[:, c, n * P:(n + 1) * P], wv_lo[:, c, n * P:(n + 1) * P],
                                             cT_hi[:, c, :], cT_lo[:, c, :], first, last)
                        elif what == "m":
                            ins = mm(dst[:, 0:AK], wq0_sb[:, c, n * P:(n + 1) * P], kT0[:, c, :], start=first, stop=last)
                        elif what == "rb0":
                            ins = mm(dst[:, 0:AK], bq0_rep[:, c, :], kT0[:, c, :], start=first, stop=last)
                        elif what == "vvs":
                            ins = nc.tensor.transpose(dst[0:KEYS, c * P:(c + 1) * P], vT0[:, c, n * KEYS:(n + 1) * KEYS], ident[:, :])
                    if what == "vvs":
                        for c in range(DC):
                            ins = mm(dst[0:KEYS, D:2 * D], vT0[:, c, n * KEYS:(n + 1) * KEYS], wsum[:, c * D:(c + 1) * D],
                                     start=c == 0, stop=c == DC - 1)
                    ins.then_inc(su_filled, 1)

            def energy(b, g, prev):
                if prev:
                    pe.wait_ge(vo_lo_ready, b * VO_FILLS)
                for i in range(GROUP):
                    for c in range(DC):
                        ins = mm(L0_BANK[g][:, i * P:(i + 1) * P], xT_sb[:, c, (g * GROUP + i) * P:(g * GROUP + i + 1) * P],
                                 m_all[:, c, bass.ds(b * KEYS, P)], start=c == 0, stop=c == DC - 1)
                ins.then_inc(energy_filled, 1)

            def g_fill(b, n, prev):
                c, k = n // 3, n % 3
                if c == 0 and prev:
                    pe.wait_ge(s_biased, 3 * b * TILES - 2 + k)
                elif c:
                    pe.wait_ge(g_lo_ready, b * 6 + n - 2)
                a, e = SCORE_PAIRS[k]
                for pr in range(a, e):
                    ins = mm(S_BANK[k][:, (pr - a) * PW:(pr - a + 1) * PW], wqT_sb[:, pr, c * P:(c + 1) * P],
                             blk_k[:, pr * PW:(pr + 1) * PW], start=True, stop=True)
                ins.then_inc(g_filled, 1)

            def attnT(b, g):
                pe.wait_ge(e_biased, b * GROUPS + g + 1)
                pe.wait_ge(attn_ready, b * GROUPS + g + 1)
                for i in range(GROUP):
                    ins = nc.tensor.transpose(L0_BANK[g][:, i * P:(i + 1) * P], attn[:, (g * GROUP + i) * P:(g * GROUP + i + 1) * P], ident[:, :])
                ins.then_inc(attnT_filled, 1)

            def l0_out(b, i):
                if i % GROUP == 0:
                    pe.wait_ge(aT_lo_ready, b * GROUPS + i // GROUP + 1)
                if i == 1:
                    pe.wait_ge(aT_lo_ready, b * GROUPS + 2)
                elif i in (2, 3):
                    pe.wait_ge(g_lo_ready, b * 6 + 3 + i)
                elif i >= NG:
                    pe.wait_ge(gated, b * TILES + i - NG + 1)
                v = bass.ds(b * BANK, BANK)
                three_pass(GATE_BANK[i % NG][:, :], aT_hi[:, i, :], aT_lo[:, i, :], vvs_hi[:, v], vvs_lo[:, v], True, True).then_inc(l0_filled, 1)

            def x1T(b, i, prev):
                pe.wait_ge(x1_ready, b * TILES + i + 1)
                if i >= NX:
                    pe.wait_ge(x1T_lo_ready, b * TILES + i - NX + 1)
                elif i == 2:
                    pe.wait_ge(g_lo_ready, b * 6 + 4)
                elif prev and i == 1:
                    pe.wait_ge(y_summed, b * TILES)
                elif prev:
                    pe.wait_ge(pT_lo_ready, 3 * b * TILES - 1)
                for c in range(DC):
                    ins = nc.tensor.transpose(X1T_BANK[i % NX][:, c * P:(c + 1) * P], xrow[:, i * D + c * P:i * D + (c + 1) * P], ident[:, :])
                ins.then_inc(x1T_filled, 1)

            def vo_fill(b, n, prev):
                if n == 0:
                    pe.wait_ge(blk_v_ready, b + 1)
                if n < 2:
                    pe.wait_ge(gated, b * TILES + TILES - NG + n + 1)
                else:
                    pe.wait_ge(vo_lo_ready, b * VO_FILLS + n - 1)
                for half in range(2):
                    c = 2 * n + half
                    dst = VO_BANK[n % 2][:, half * D:(half + 1) * D]
                    pairs = [pr for pr in range(PAIRS) if pr * PW < (c + 1) * P and (pr + 1) * PW > c * P]
                    for pr in pairs:
                        at = P + pr * VSTRIDE + c * P - pr * PW
                        ins = mm(dst, blk_v[:, at:at + P], wo_sb[:, pr, :], start=pr == pairs[0], stop=c > 0 and pr == pairs[-1])
                    if c == 0:
                        ins = mm(dst, sel_h0[:, :], bo_sb[:, :], start=False, stop=True)
                ins.then_inc(vo_filled, 1)

            def scores(b, s, k, first_tile_of_batch):
                if k == 0:
                    pe.wait_ge(x1T_lo_ready, b * TILES + s + 1)
                if first_tile_of_batch:
                    if k == 0:
                        pe.wait_ge(g_lo_ready, (b + 1) * 6)
                        pe.wait_ge(x1T_lo_ready, b * TILES + X1T_IN_S0 + 1)
                    else:
                        pe.wait_ge(gated, (b + 1) * TILES)
                else:
                    pe.wait_ge(s_biased, 3 * (b * TILES + s) - 2 + k)
                a, e = SCORE_COLS[k]
                for c in range(DC):
                    ins = three_pass(S_BANK[k][:, 0:e - a], x1T_hi[:, s, c * P:(c + 1) * P], x1T_lo[:, s, c * P:(c + 1) * P],
                                     g_hi[:, c, a:e], g_lo[:, c, a:e], c == 0, c == DC - 1)
                ins.then_inc(scores_filled, 1)

            def pT(b, s, k, prev=True):
                at = 3 * (b * TILES + s)
                if k < 2:
                    pe.wait_ge(probs_ready, 2 * (b * TILES + s) + k + 1)
                if k == 2:
                    pe.wait_ge(pT_lo_ready, at + 1)
                elif s == 0 and k == 1:
                    pe.wait_ge(x1T_lo_ready, (b + 1) * TILES)
                elif prev or s > 0:
                    pe.wait_ge(pT_lo_ready, at - (0 if k == 0 else 1))
                c0, c1 = PT_FILLS[k]
                for c in range(c0, c1):
                    ins = nc.tensor.transpose(T_BANK[PT_BANK[k]][:, (c - c0) * P:(c - c0 + 1) * P],
                                              f_slot(s, c * P, (c + 1) * P), ident[:, :])
                ins.then_inc(pT_filled, 1)

            def pv(b, s, k):
                pe.wait_ge(pT_lo_ready, 3 * (b * TILES + s) + k + 1)
                if k == 0 and s == 0:
                    pe.wait_ge(vo_lo_ready, (b + 1) * VO_FILLS)
                elif k == 0:
                    pe.wait_ge(y_summed, b * TILES + s)
                c0, c1 = PT_FILLS[k]
                for c in range(c0, c1):
                    ins = three_pass(O_BANK[:, 0:D], pt_hi[:, c, :], pt_lo[:, c, :], vo_hi[:, c, :], vo_lo[:, c, :], c == 0, c == CH - 1)
                if k == 2:
                    ins.then_inc(out_filled, 1)

            def head(b, prev, cur):
                if cur:
                    pe.wait_ge(xT_loaded, 16 * (b + 1))
                    energy(b, 0, prev)
                    energy(b, 1, prev)
                if prev:
                    pT(b - 1, 6, 0)
                    pT(b - 1, 6, 1)
                if cur:
                    pe.wait_ge(blk_k_ready, b + 1)
                    for n in range(3):
                        g_fill(b, n, prev)
                if prev:
                    pT(b - 1, 6, 2)
                    pv(b - 1, 6, 0)
                if cur:
                    attnT(b, 0)
                if cur:
                    for n in range(3, 6):
                        g_fill(b, n, prev)
                    attnT(b, 1)
                if prev:
                    pv(b - 1, 6, 1)
                    pv(b - 1, 6, 2)
                    pT(b - 1, 7, 0)
                if cur:
                    l0_out(b, 0)
                    l0_out(b, 1)
                    l0_out(b, 2)
                if prev:
                    pT(b - 1, 7, 1)
                    pT(b - 1, 7, 2)
                    pv(b - 1, 7, 0)
                if cur:
                    l0_out(b, 3)
                if prev:
                    pv(b - 1, 7, 1)
                    pv(b - 1, 7, 2)
                if cur:
                    for i in range(L0_EARLY, TILES):
                        l0_out(b, i)
                        for j in X1T_AFTER[i]:
                            x1T(b, j, prev)
                    vo_fill(b, 0, prev)
                    x1T(b, X1T_LATE[0], prev)

            def batch(b, prev):
                head(b, prev, True)
                for s in range(TILES):
                    if s == 0:
                        scores(b, 0, 0, True)
                        x1T(b, X1T_LATE[1], prev)
                        scores(b, 0, 1, True)
                        scores(b, 0, 2, True)
                        vo_fill(b, 1, prev)
                        continue
                    if s == 1:
                        for k in range(3):
                            scores(b, 1, k, False)
                        for n in (2, 3, 4):
                            vo_fill(b, n, prev)
                        continue
                    pT(b, s - 2, 0, prev)
                    scores(b, s, 0, False)
                    pT(b, s - 2, 1)
                    scores(b, s, 1, False)
                    pT(b, s - 2, 2)
                    pv(b, s - 2, 0)
                    scores(b, s, 2, False)
                    pv(b, s - 2, 1)
                    pv(b, s - 2, 2)

            setup()
            pe.wait_ge(*evacuated(N_SETUP - 8 + 3))
            pe.wait_ge(pads_set, N_PADS)
            pe.wait_ge(ld_w1, 32)
            batch(0, False)
            with pe.Fori(1, NB) as b:
                batch(b, True)
            head(NB, True, False)

        @block.scalar
        def _(act):
            copy = nc.scalar.copy
            act.dma_start(cols_sb[:, :], cols).then_inc(ld_cols, 16)
            act.dma_start(ident[:, :], ident_in).then_inc(ld_ident, 16)
            act.dma_start(small[:, 0:1], gamma.partition_broadcast(P)).then_inc(ld_vec, 16)
            act.dma_start(bias_rows, rows[R_B1:R_B3 + 1, :].partition_broadcast(P)).then_inc(ld_vec, 16)
            act.dma_start(bo_sb[:, :], bo).then_inc(ld_vec, 16)
            act.dma_start(ln_gb[:, :, :], rows[R_LNG:R_LNB + 1, :].partition_broadcast(P)).then_inc(ld_vec, 16)

            def setup():
                act.wait_ge(ld_cols, 16)
                for c in range(DC):
                    ins = copy(bq0_rep[:, c, :], cols_sb[:, C_BQ0 + c:C_BQ0 + c + 1].broadcast_to([P, P]))
                ins.then_inc(consts_set, 1)
                act.wait_ge(pads_set, N_PADS_EARLY)
                for i, (what, n, who) in enumerate(SETUP):
                    src = ps[i % 8][:, 0:AK]
                    if what == "vvs":
                        act.wait_ge(*evacuated(i))
                        copy(vvs_hi[0:KEYS, n * BANK:(n + 1) * BANK], vvs_raw[n % 2]).then_inc(vvs_hi_ready, 1)
                        continue
                    if who != "act":
                        if what == "rb0":
                            copy(cT_hi, cT_sb).then_inc(cT_hi_ready, 1)
                            for loaded, raw, hi in ((ld_wk, wk_sb, wk_hi), (ld_wv, wv_sb, wv_hi)):
                                act.wait_ge(loaded, 16)
                                for a, e in W_HALVES:
                                    copy(hi[:, :, a:e], raw[:, :, a:e]).then_inc(w_hi_ready, 1)
                        continue
                    act.wait_ge(su_filled, i + 1)
                    if what == "kT0":
                        ins = nc.scalar.activation(kT0[:, n, :], src, ACT.Identity, bias=cols_sb[:, C_BK0 + n:C_BK0 + n + 1])
                    elif what == "kh":
                        if n == 0:
                            act.wait_ge(wsum_ready, 1)
                        ins = nc.scalar.activation(kh_all[:, n, :], src, ACT.Identity, bias=bk8[:, n:n + 1], scale=SCALE)
                    else:
                        ins = copy(m_all[:, n, 0:AK], src)
                    ins.then_inc(su_act, 1)
            def g_split(b, n):
                c, k = n // 3, n % 3
                a, e = SCORE_COLS[k]
                act.wait_ge(g_filled, b * 6 + n + 1)
                copy(g_hi[:, c, a:e], S_BANK[k][:, 0:e - a]).then_inc(g_hi_ready, 1)

            def vo_split(b, n):
                act.wait_ge(vo_filled, b * VO_FILLS + n + 1)
                copy(vo_hi[:, 2 * n:2 * n + 2, :].rearrange("p c n -> p (c n)"), VO_BANK[n % 2][:, :]).then_inc(vo_hi_ready, 1)

            def exp0(b, g):
                act.wait_ge(negmax0_ready, b * GROUPS + g + 1)
                for i in range(g * GROUP, (g + 1) * GROUP):
                    e = attn[:, i * P:i * P + KEYS]
                    ins = nc.scalar.activation(e, e, ACT.Exp, bias=negmax0[:, i:i + 1], accum_out=sums0[:, i:i + 1])
                ins.then_inc(exp0_done, 1)

            def aT_split(b, g):
                act.wait_ge(attnT_filled, b * GROUPS + g + 1)
                copy(aT_hi[:, g * GROUP:(g + 1) * GROUP, :].rearrange("p i n -> p (i n)"), L0_BANK[g][:, :]).then_inc(aT_hi_ready, 1)

            def tanh(b, i):
                act.wait_ge(l0_filled, b * TILES + i + 1)
                if i >= 2:
                    act.wait_ge(gated, b * TILES + i - 1)
                nc.scalar.activation(th[:, i % 2, :], GATE_BANK[i % NG][:, D:2 * D], ACT.Tanh, scale=0.5).then_inc(tanh_ready, 1)

            def x1T_split(b, i):
                act.wait_ge(x1T_filled, b * TILES + i + 1)
                copy(x1T_hi[:, i, :], X1T_BANK[i % NX][:, 0:D]).then_inc(x1T_hi_ready, 1)

            def pT_split(b, s, k):
                c0, c1 = PT_FILLS[k]
                act.wait_ge(pT_filled, 3 * (b * TILES + s) + k + 1)
                copy(pt_hi[:, c0:c1, :].rearrange("p c n -> p (c n)"), T_BANK[PT_BANK[k]][:, 0:(c1 - c0) * P]).then_inc(pT_hi_ready, 1)

            def exp(b, s, h0, h1):
                if h0 == 0:
                    act.wait_ge(negmax_ready, b * TILES + s + 1)
                for h in range(h0, h1):
                    e = f_slot(s, h * KEYS, (h + 1) * KEYS)
                    ins = nc.scalar.activation(e, e, ACT.Exp, bias=negmax[:, s % 2, h:h + 1], accum_out=sums[:, s % 2, h:h + 1])
                    if h + 1 in (HALVES[0][1], HALVES[1][1]):
                        ins.then_inc(exp_done, 1)

            def head(b, prev, cur):
                if prev and cur:
                    exp(b - 1, 7, 0, 8)
                    exp0(b, 0)
                    pT_split(b - 1, 6, 0)
                    pT_split(b - 1, 6, 1)
                elif prev:
                    for k in range(2):
                        exp(b - 1, 7, 4 * k, 4 * k + 4)
                        pT_split(b - 1, 6, k)
                else:
                    exp0(b, 0)
                if cur:
                    for n in range(3):
                        g_split(b, n)
                if prev:
                    pT_split(b - 1, 6, 2)
                if cur:
                    exp0(b, 1)
                    aT_split(b, 0)
                for n in range(3, 6):
                    if prev:
                        exp(b - 1, 7, *EXP7_SPLIT[n - 3:n - 1])
                    if cur:
                        g_split(b, n)
                if cur:
                    aT_split(b, 1)
                if prev:
                    exp(b - 1, 7, EXP7_SPLIT[3], HEADS)
                    pT_split(b - 1, 7, 0)
                if cur:
                    tanh(b, 0)
                    tanh(b, 1)
                if prev:
                    pT_split(b - 1, 7, 1)
                    pT_split(b - 1, 7, 2)
                if cur:
                    tanh(b, 2)
                    tanh(b, 3)
                    for i in range(L0_EARLY, TILES):
                        tanh(b, i)
                        for j in X1T_AFTER[i]:
                            x1T_split(b, j)
                    vo_split(b, 0)
                    for j in X1T_LATE:
                        x1T_split(b, j)

            def batch(b, prev):
                head(b, prev, True)
                for s in range(TILES):
                    if s == 0:
                        vo_split(b, 1)
                        exp(b, 0, 0, 12)
                        vo_split(b, 2)
                        exp(b, 0, 12, HEADS)
                        vo_split(b, 3)
                        exp(b, 1, 0, 3)
                        vo_split(b, 4)
                        continue
                    if s == 1:
                        continue
                    parts = [3, 4, 6, 8, HEADS] if s == 2 else [0, 2, 5, 8, HEADS]
                    for k in range(3):
                        exp(b, s - 1, *parts[k:k + 2])
                        pT_split(b, s - 2, k)
                    exp(b, s - 1, *parts[3:])

            setup()
            act.wait_ge(vvs_lo_ready, NB)
            act.wait_ge(pads_set, N_PADS)
            batch(0, False)
            with act.Fori(1, NB) as b:
                batch(b, True)
            head(NB, True, False)

        @block.vector
        def _(dve):
            v = nc.vector

            def setup():
                dve.wait_ge(ld_cols, 16)
                v.tensor_scalar(bk8[:, :], cols_sb[:, C_BK1:C_BK1 + PAIRS], SCALE, None, ALU.mult).then_inc(wsum_ready, 1)
                dve.wait_ge(pads_set, 1)
                v.tensor_copy(bq_blk[0:DK, 0:P:HEADS + 2], cols_sb[0:DK, C_BQ1:C_BQ1 + PAIRS])
                v.tensor_copy(bq_blk[DK:P, 1:P:HEADS + 2], cols_sb[DK:P, C_BQ1:C_BQ1 + PAIRS]).then_inc(bq_ready, 1)
                for i, (what, n, who) in enumerate(SETUP):
                    if who != "dve":
                        continue
                    if what == "rb0":
                        sums_of_weights()
                        dve.wait_ge(cT_hi_ready, 1)
                        v.tensor_tensor(cT_lo, cT_sb, cT_hi, ALU.subtract).then_inc(cT_lo_ready, 1)
                    src = ps[i % 8][:, 0:AK]
                    dve.wait_ge(su_filled, i + 1)
                    if what == "vT0":
                        ins = v.tensor_scalar(vT0[:, n, :], src, cols_sb[:, C_BV0 + n:C_BV0 + n + 1], None, ALU.add)
                    elif what == "vh":
                        ins = v.tensor_scalar(vh_all[:, n, :], src, cols_sb[:, C_BV1 + n:C_BV1 + n + 1], None, ALU.add)
                    elif what == "rb0":
                        ins = v.tensor_copy(rb0[:, :], src)
                    elif what == "rb1":
                        ins = v.tensor_scalar(rb_all[:, :], ps[i % 8][0:HEADS, 0:AK], 0.5, None, ALU.mult)
                    else:
                        if n >= 2:
                            dve.wait_ge(vvs_lo_ready, n - 1)
                        v.tensor_scalar(vvs_raw[n % 2][:, 0:D], ps[i % 8][0:KEYS, 0:D], small[0:KEYS, 0:1], None, ALU.mult).then_inc(vvs_chain, 1)
                        v.tensor_tensor(vvs_raw[n % 2][:, D:2 * D], ps[i % 8][0:KEYS, D:2 * D], bias_rows[0:KEYS, 0, :],
                                        ALU.add).then_inc(su_dve, 1)
                        if n:
                            vvs_split(n - 1)
                        if n == NB - 1:
                            vvs_split(n)
                        continue
                    ins.then_inc(su_dve, 1)

            def sums_of_weights():
                dve.wait_ge(ld_w123, 48)
                v.tensor_tensor(wsum, w123[:, 0, :], w123[:, 1, :], ALU.add).then_inc(vvs_chain, 1)
                dve.wait_ge(vvs_chain, 1)
                v.tensor_tensor(wsum, wsum, w123[:, 2, :], ALU.add).then_inc(wsum_ready, 1)
                dve.wait_ge(ld_vec, 64)
                v.tensor_scalar(small[:, 0:1], small[:, 0:1], 0.5, None, ALU.mult).then_inc(vvs_chain, 1)
                v.tensor_tensor(bias_rows[:, 0, :], bias_rows[:, 0, :], bias_rows[:, 1, :], ALU.add).then_inc(vvs_chain, 1)
                dve.wait_ge(vvs_chain, 3)
                v.tensor_tensor(bias_rows[:, 0, :], bias_rows[:, 0, :], bias_rows[:, 2, :], ALU.add).then_inc(vvs_chain, 1)
                dve.wait_ge(vvs_chain, 4)
                dve.wait_ge(pads_set, N_PADS_EARLY)

            def vvs_split(n):
                dve.wait_ge(vvs_hi_ready, n + 1)
                v.tensor_tensor(vvs_lo[0:KEYS, n * BANK:(n + 1) * BANK], vvs_raw[n % 2],
                                vvs_hi[0:KEYS, n * BANK:(n + 1) * BANK], ALU.subtract).then_inc(vvs_lo_ready, 1)

            def blk_k_copy(b, prev):
                if prev:
                    dve.wait_ge(g_filled, 6 * b)
                view = blk_k[:, :].rearrange("p (r n) -> p r n", r=PAIRS)
                v.tensor_copy(view[0:DK, :, 0:KEYS], kh_all[0:DK, :, bass.ds(b * KEYS, KEYS)])
                v.tensor_copy(view[DK:P, :, KEYS:PW], kh_all[DK:P, :, bass.ds(b * KEYS, KEYS)]).then_inc(blk_k_ready, 1)

            def blk_v_copy(b, prev):
                if prev:
                    dve.wait_ge(vo_filled, b * VO_FILLS)
                view = blk_v[:, P:].rearrange("p (r n) -> p r n", r=PAIRS)
                v.tensor_copy(view[0:DK, :, 0:KEYS], vh_all[0:DK, :, bass.ds(b * KEYS, KEYS)])
                v.tensor_copy(view[DK:P, :, KEYS:PW], vh_all[DK:P, :, bass.ds(b * KEYS, KEYS)]).then_inc(blk_v_ready, 1)

            def energy(b, g):
                e = attn[:, g * GROUP * P:(g + 1) * GROUP * P].rearrange("p (i n) -> p i n", i=GROUP)[:, :, 0:KEYS]
                dve.wait_ge(energy_filled, b * GROUPS + g + 1)
                v.tensor_tensor(e, L0_BANK[g][:, :].rearrange("p (i n) -> p i n", i=GROUP)[:, :, 0:KEYS],
                                rb0[:, bass.ds(b * KEYS, KEYS)].unsqueeze(1).broadcast_to([P, GROUP, KEYS]), ALU.add).then_inc(e_biased, 1)
                dve.wait_ge(e_biased, b * GROUPS + g + 1)
                v.tensor_reduce(negmax0[:, g * GROUP:(g + 1) * GROUP], e, AX.X, ALU.max, negate=True).then_inc(negmax0_ready, 1)

            def rsum0_of(b, g):
                dve.wait_ge(exp0_done, b * GROUPS + g + 1)
                v.reciprocal(rsum0[:, g * GROUP:(g + 1) * GROUP], sums0[:, g * GROUP:(g + 1) * GROUP]).then_inc(rsum0_ready, 1)

            def g_split(b, n):
                c, k = n // 3, n % 3
                a, e = SCORE_COLS[k]
                dve.wait_ge(g_hi_ready, b * 6 + n + 1)
                v.tensor_tensor(g_lo[:, c, a:e], S_BANK[k][:, 0:e - a], g_hi[:, c, a:e], ALU.subtract).then_inc(g_lo_ready, 1)

            def aT_split(b, g):
                dve.wait_ge(aT_hi_ready, b * GROUPS + g + 1)
                sl = slice(g * GROUP, (g + 1) * GROUP)
                v.tensor_tensor(aT_lo[:, sl, :].rearrange("p i n -> p (i n)"), L0_BANK[g][:, :],
                                aT_hi[:, sl, :].rearrange("p i n -> p (i n)"), ALU.subtract).then_inc(aT_lo_ready, 1)

            def gate(b, i, prev):
                dve.wait_ge(tanh_ready, b * TILES + i + 1)
                if i >= 2 or prev:
                    dve.wait_ge(x1_ready, b * TILES + i - 1)
                v.scalar_tensor_tensor(out=o_sb[:, i % 2, :], in0=th[:, i % 2, :], scalar=1.0, in1=GATE_BANK[i % NG][:, 0:D],
                                       op0=ALU.add, op1=ALU.mult).then_inc(gated, 1)

            def x1T_split(b, i):
                dve.wait_ge(x1T_hi_ready, b * TILES + i + 1)
                v.tensor_tensor(x1T_lo[:, i, :], X1T_BANK[i % NX][:, 0:D], x1T_hi[:, i, :], ALU.subtract).then_inc(x1T_lo_ready, 1)

            def vo_split(b, n):
                dve.wait_ge(vo_hi_ready, b * VO_FILLS + n + 1)
                v.tensor_tensor(vo_lo[:, 2 * n:2 * n + 2, :].rearrange("p c n -> p (c n)"), VO_BANK[n % 2][:, :],
                                vo_hi[:, 2 * n:2 * n + 2, :].rearrange("p c n -> p (c n)"), ALU.subtract).then_inc(vo_lo_ready, 1)

            def s_bias(b, s, k):
                a, e = SCORE_COLS[k]
                if k == 0:
                    dve.wait_ge(f_biased, b * TILES + s + 1)
                dve.wait_ge(scores_filled, 3 * (b * TILES + s) + k + 1)
                v.scalar_tensor_tensor(out=f_slot(s, a, e), in0=f_slot(s, a, e), scalar=2.0, in1=S_BANK[k][:, 0:e - a],
                                       op0=ALU.mult, op1=ALU.add).then_inc(s_biased, 1)

            def s_max(b, s):
                dve.wait_ge(s_biased, 3 * (b * TILES + s + 1))
                v.tensor_reduce(negmax[:, s % 2, :], f_slot(s).rearrange("p (h n) -> p h n", h=HEADS), AX.X, ALU.max,
                                negate=True).then_inc(negmax_ready, 1)

            def recip(b, s, half):
                h0, h1 = HALVES[half]
                dve.wait_ge(exp_done, 2 * (b * TILES + s) + half + 1)
                v.reciprocal(rsum[:, s % 2, h0:h1], sums[:, s % 2, h0:h1]).then_inc(rsum_ready, 1)

            def pT_split(b, s, k):
                c0, c1 = PT_FILLS[k]
                dve.wait_ge(pT_hi_ready, 3 * (b * TILES + s) + k + 1)
                v.tensor_tensor(pt_lo[:, c0:c1, :].rearrange("p c n -> p (c n)"), T_BANK[PT_BANK[k]][:, 0:(c1 - c0) * P],
                                pt_hi[:, c0:c1, :].rearrange("p c n -> p (c n)"), ALU.subtract).then_inc(pT_lo_ready, 1)

            def ln_stats(b, s, may_be_first):
                t = b * TILES + s
                if not (may_be_first and s < YSLOTS):
                    dve.wait_ge(out_stored[s % YSLOTS], 16 * (TILES // YSLOTS) * b + 16 * (s // YSLOTS))
                dve.wait_ge(out_filled, t + 1)
                yt = y[:, s % YSLOTS, :]
                v.tensor_tensor(yt, O_BANK[:, 0:D], xrow[:, s * D:(s + 1) * D], ALU.add).then_inc(y_summed, 1)
                dve.wait_ge(y_summed, t + 1)
                v.bn_stats(stats[:, :], yt).then_inc(y_stats, 1)
                dve.wait_ge(ld_vec, 64)
                dve.wait_ge(y_stats, t + 1)
                v.bn_aggr(meanvar[:, s % YSLOTS, :], stats[:, :]).then_inc(y_meanvar, 1)
                dve.wait_ge(y_meanvar, t + 1)
                v.tensor_scalar(var_eps[:, s % YSLOTS:s % YSLOTS + 1], meanvar[:, s % YSLOTS, 1:2], EPS, None, ALU.add).then_inc(var_ready, 1)

            def ln_norm(b, s):
                yt = y[:, s % YSLOTS, :]
                dve.wait_ge(rstd_ready, b * TILES + s + 1)
                v.tensor_scalar(yt, yt, meanvar[:, s % YSLOTS, 0:1], rstd[:, s % YSLOTS:s % YSLOTS + 1],
                                ALU.subtract, ALU.mult).then_inc(y_normed, 1)

            def ln_affine_last(b):
                yt = y[:, (TILES - 1) % YSLOTS, :]
                dve.wait_ge(y_normed, (b + 1) * TILES)
                v.tensor_tensor(yt, yt, ln_gb[:, 0, :], ALU.mult).then_inc(y_scaled, 1)
                dve.wait_ge(y_scaled, (b + 1) * TILES)
                v.tensor_tensor(yt, yt, ln_gb[:, 1, :], ALU.add).then_inc(y_final, 1)

            def head(b, prev, cur):
                if cur:
                    blk_k_copy(b, prev)
                    energy(b, 0)
                    energy(b, 1)
                if prev:
                    pT_split(b - 1, 6, 0)
                if cur:
                    rsum0_of(b, 0)
                if prev:
                    recip(b - 1, 7, 0)
                    pT_split(b - 1, 6, 1)
                if cur:
                    for n in range(3):
                        g_split(b, n)
                if prev:
                    pT_split(b - 1, 6, 2)
                    ln_norm(b - 1, 5)
                if cur:
                    rsum0_of(b, 1)
                    aT_split(b, 0)
                    for n in range(3, 6):
                        g_split(b, n)
                    aT_split(b, 1)
                if prev:
                    recip(b - 1, 7, 1)
                    pT_split(b - 1, 7, 0)
                    ln_stats(b - 1, 6, False)
                if cur:
                    gate(b, 0, prev)
                    gate(b, 1, prev)
                if prev:
                    pT_split(b - 1, 7, 1)
                    pT_split(b - 1, 7, 2)
                    ln_norm(b - 1, 6)
                if cur:
                    gate(b, 2, prev)
                    blk_v_copy(b, prev)
                    gate(b, 3, prev)
                if prev:
                    ln_stats(b - 1, 7, False)
                if cur:
                    for i in range(L0_EARLY, TILES):
                        gate(b, i, prev)
                        for j in X1T_AFTER[i]:
                            x1T_split(b, j)
                    vo_split(b, 0)
                    x1T_split(b, X1T_LATE[0])
                    if prev:
                        ln_norm(b - 1, 7)
                    x1T_split(b, X1T_LATE[1])
                elif prev:
                    ln_norm(b - 1, 7)
                    ln_affine_last(b - 1)

            def batch(b, prev):
                head(b, prev, True)
                for s in range(TILES):
                    if s < 2:
                        if s == 0:
                            for k in range(3):
                                s_bias(b, 0, k)
                            s_max(b, 0)
                            vo_split(b, 1)
                        else:
                            s_bias(b, 1, 0)
                            s_bias(b, 1, 1)
                            recip(b, 0, 0)
                            s_bias(b, 1, 2)
                            s_max(b, 1)
                            vo_split(b, 2)
                            vo_split(b, 3)
                            recip(b, 0, 1)
                            vo_split(b, 4)
                        continue
                    pT_split(b, s - 2, 0)
                    s_bias(b, s, 0)
                    pT_split(b, s - 2, 1)
                    if s > 2:
                        ln_norm(b, s - 3)
                    s_bias(b, s, 1)
                    pT_split(b, s - 2, 2)
                    recip(b, s - 1, 0)
                    s_bias(b, s, 2)
                    s_max(b, s)
                    recip(b, s - 1, 1)
                    ln_stats(b, s - 2, not prev)

            setup()
            dve.wait_ge(su_filled, N_SETUP)
            dve.wait_ge(*evacuated(FILL_OF["kh", PAIRS - 1]))
            dve.wait_ge(pads_set, N_PADS)
            batch(0, False)
            with dve.Fori(1, NB) as b:
                batch(b, True)
            head(NB, True, False)

        @block.gpsimd
        def _(pool):
            g_ = nc.gpsimd

            def f_bias(b, s):
                pool.wait_ge(f_loaded[s % SLOTS], 16 * ((TILES // SLOTS) * b + s // SLOTS + 1))
                if s == 0:
                    pool.wait_ge(rb_loaded, 16 * (b + 1))
                g_.tensor_tensor(f_slot(s), f_slot(s), rb1[:, :], ALU.add).then_inc(f_biased, 1)

            def normalise(b, s, half):
                h0, h1 = HALVES[half]
                pool.wait_ge(rsum_ready, 2 * (b * TILES + s) + half + 1)
                p = f_slot(s, h0 * KEYS, h1 * KEYS).rearrange("p (h n) -> p h n", n=KEYS)
                g_.tensor_tensor(p, p, rsum[:, s % 2, h0:h1].unsqueeze(2).broadcast_to([P, h1 - h0, KEYS]), ALU.mult).then_inc(probs_ready, 1)

            def normalise0(b, g):
                pool.wait_ge(rsum0_ready, b * GROUPS + g + 1)
                e = attn[:, g * GROUP * P:(g + 1) * GROUP * P].rearrange("p (i n) -> p i n", i=GROUP)[:, :, 0:KEYS]
                g_.tensor_tensor(e, e, rsum0[:, g * GROUP:(g + 1) * GROUP].unsqueeze(2).broadcast_to([P, GROUP, KEYS]),
                                 ALU.mult).then_inc(attn_ready, 1)

            def x1(b, i):
                for g, (t0, _) in enumerate(X_PIECES):
                    if i == t0:
                        pool.wait_ge(x_loaded[g], 16 * (b + 1))
                pool.wait_ge(gated, b * TILES + i + 1)
                xt = xrow[:, i * D:(i + 1) * D]
                g_.tensor_tensor(xt, xt, o_sb[:, i % 2, :], ALU.add).then_inc(x1_ready, 1)

            def rstd_of(b, s):
                pool.wait_ge(var_ready, b * TILES + s + 1)
                j = s % YSLOTS
                g_.tensor_tensor(rstd[:, j:j + 1], var_eps[:, j:j + 1], small[:, 1:2], ALU.pow).then_inc(rstd_ready, 1)

            def ln_affine(b, s):
                yt = y[:, s % YSLOTS, :]
                pool.wait_ge(y_normed, b * TILES + s + 1)
                g_.tensor_tensor(yt, yt, ln_gb[:, 0, :], ALU.mult).then_inc(y_scaled, 1)
                pool.wait_ge(y_scaled, b * TILES + s + 1)
                g_.tensor_tensor(yt, yt, ln_gb[:, 1, :], ALU.add).then_inc(y_final, 1)

            def head(b, prev, cur):
                if prev:
                    normalise(b - 1, 6, 0)
                    normalise(b - 1, 6, 1)
                    rstd_of(b - 1, 5)
                if cur:
                    normalise0(b, 0)
                if prev:
                    normalise(b - 1, 7, 0)
                if cur:
                    normalise0(b, 1)
                    f_bias(b, 0)
                if prev:
                    normalise(b - 1, 7, 1)
                    ln_affine(b - 1, 5)
                    rstd_of(b - 1, 6)
                if cur:
                    for i in range(TILES):
                        x1(b, i)
                        if i == 1 and prev:
                            ln_affine(b - 1, 6)
                        if i == 4 and prev:
                            rstd_of(b - 1, 7)
                else:
                    ln_affine(b - 1, 6)
                    rstd_of(b - 1, 7)

            def batch(b, prev):
                head(b, prev, True)
                for s in range(TILES):
                    if s > 2:
                        rstd_of(b, s - 3)
                    if s + 1 < TILES:
                        f_bias(b, s + 1)
                    if s == 0 and prev:
                        ln_affine(b - 1, 7)
                    if s > 2:
                        ln_affine(b, s - 3)
                    if 0 < s < TILES - 1:
                        normalise(b, s - 1, 0)
                        normalise(b, s - 1, 1)

            g_.memset(warm, 0.0).then_inc(warm_ready, 1)
            g_.memset(bq_blk[:, :], 0.0).then_inc(pads_set, 1)
            g_.memset(small[:, 1:2], -0.5).then_inc(pads_set, 1)
            g_.memset(sel_h0[:, :], 0.0).then_inc(pool_chain, 1)
            pool.wait_ge(pool_chain, 1)
            g_.memset(sel_h0[:, 0:KEYS], 1.0).then_inc(pads_set, 1)
            g_.memset(vvs_hi[:, :].bitcast(F32), 0.0).then_inc(pads_set, 1)
            g_.memset(vvs_lo[:, :].bitcast(F32), 0.0).then_inc(pads_set, 1)
            g_.memset(m_all[:, :, AK:], 0.0).then_inc(pads_set, 1)
            g_.memset(fs_slots[:, :, HK:], 0.0).then_inc(pads_set, 1)
            for i, (raw, hi, lo) in enumerate(((wk_sb, wk_hi, wk_lo), (wv_sb, wv_hi, wv_lo))):
                for j, (a, e) in enumerate(W_HALVES):
                    pool.wait_ge(w_hi_ready, 2 * i + j + 1)
                    g_.tensor_tensor(lo[:, :, a:e], raw[:, :, a:e], hi[:, :, a:e], ALU.subtract).then_inc(w_lo_ready, 1)
            pool.wait_ge(su_filled, VVS_DONE)
            pool.wait_ge(vvs_lo_ready, NB)
            g_.memset(blk_k[:, :], 0.0).then_inc(pads_set, 1)
            g_.memset(attn[:, :].rearrange("p (i n) -> p i n", i=TILES)[:, :, KEYS:], 0.0).then_inc(pads_set, 1)
            g_.memset(blk_v[:, :], 0.0).then_inc(pads_set, 1)
            batch(0, False)
            with pool.Fori(1, NB) as b:
                batch(b, True)
            head(NB, True, False)


_OUT = (NB, SEQ, D)


def kernel(**inputs):
    import numpy as np
    import concourse.bacc as bacc
    from concourse.bass_utils import run_bass_kernel_spmd

    a = {k: np.asarray(v) for k, v in inputs.items()}
    l0 = {k[9:]: v for k, v in a.items() if k.startswith("L0_xattn_")}
    l1 = {k[9:]: v for k, v in a.items() if k.startswith("L1_xattn_")}
    x = a["x"].reshape(NB * SEQ, D)
    chunks = [v.reshape(-1, P).T for v in (l0["bk"], l0["bv"], l0["bq"], l1["bq"], l1["bk"], l1["bv"])]
    arrays = {
        "x": x, "xT": x.T, "cT": a["ctx_1024"].reshape(AK, D).T,
        "fside": a["fside_Bx16xSxS2_0"].transpose(0, 2, 1, 3).reshape(NB * SEQ, HK),
        "wq0": l0["Wq"], "wk0T": l0["Wk"].T, "wv0T": l0["Wv"].T,
        "w1T": l0["W1"].T, "w2T": l0["W2"].T, "w3T": l0["W3"].T,
        "wqT": l1["wq"].T, "wk": l1["wk"], "wv": l1["wv"], "wo": l1["wo"],
        "cols": np.concatenate(chunks, axis=1),
        "rows": np.stack([l0["b1"], l0["b2"], l0["b3"], l1["ln_g"], l1["ln_b"]]),
        "bo": l1["bo"].reshape(1, D), "gamma": l0["gamma"].reshape(1), "ident_in": np.eye(P, dtype=np.float32),
    }
    arrays = {f"in_{k}": np.ascontiguousarray(v) for k, v in arrays.items()}
    nc = bacc.Bacc("TRN2", target_bir_lowering=False, num_devices=1)
    args = [nc.dram_tensor(k, v.shape, mybir.dt.from_np(v.dtype), kind="ExternalInput").ap() for k, v in arrays.items()]
    args.append(nc.dram_tensor("out_0", (NB * SEQ, D), F32, kind="ExternalOutput").ap())
    build(nc, *args, nc.dram_tensor("rb_rows", (NB, HK), F32, kind="Internal").ap())
    r = run_bass_kernel_spmd(nc, [arrays], core_ids=[0])
    return r.results[0]["out_0"].reshape(_OUT)
```

```python
from contextlib import ExitStack

import concourse.bass as bass
from concourse import mybir

F32 = mybir.dt.float32
F32R = mybir.dt.float32r
ALU = mybir.AluOpType
ACT = mybir.ActivationFunctionType
AX = mybir.AxisListType

P = 128
NB, SEQ, D = 4, 1024, 256
KEYS, HEADS, DK = 77, 16, 64
DC = D // P
TILES = SEQ // P
GROUP = 4
GROUPS = TILES // GROUP
X_PIECES = [(0, 4), (4, 7), (7, 8)]
PAIRS = HEADS // 2
HK = HEADS * KEYS
HKP = -(-HK // P) * P
CH = HKP // P
PW = 2 * KEYS
AK = NB * KEYS
BANK = 512
SCORE_PAIRS = [(0, 3), (3, 6), (6, 8)]
EARLY_HEADS = 2 * SCORE_PAIRS[0][1]
SCORE_COLS = [(a * PW, b * PW) for a, b in SCORE_PAIRS]
PT_FILLS = [(0, 4), (4, 8), (8, 10)]
PT_BANK = [0, 1, 0]
HALVES = [(0, HEADS // 2), (HEADS // 2, HEADS)]
W_HALVES = [(h0 * DK, h1 * DK) for h0, h1 in HALVES]
SLOTS = 4
YSLOTS = 4
VSTRIDE = PW + P
VWIDTH = PAIRS * VSTRIDE
ONE_ROW = 96
SCALE = DK ** -0.5
EPS = 1e-6
VO_FILLS = CH // 2
V_FIRST = TILES * D // AK
WARM_UPS = 8
L0_EARLY = 4
X1T_AFTER = {4: [0], 5: [1, 2], 6: [3], 7: [4, 5]}
X1T_LATE = [6, 7]
EXP7_SPLIT = [8, 10, 11, 12]
assert SCALE == 0.125 and CH == PT_FILLS[-1][1]
C_BK0, C_BV0, C_BQ0, C_BQ1, C_BK1, C_BV1 = 0, 2, 4, 6, 14, 22
NCOLS = 30
R_B1, R_B2, R_B3, R_LNG, R_LNB = range(5)


def build(nc, x, xT, cT, fside, wq0, wk0T, wv0T, w1T, w2T, w3T, wqT, wk, wv, wo, cols, rows, bo, gamma, ident_in, out, rb_dram, v_dram):
    x_v = x.rearrange("(b t p) d -> p b t d", b=NB, t=TILES)
    xT_v = xT.rearrange("(c p) n -> p c n", p=P)
    f_v = fside.rearrange("(t p) n -> p t n", p=P)
    out_v = out.rearrange("(t p) n -> p t n", p=P)

    with ExitStack() as ctx:
        def sb(name, shape, dt=F32):
            return ctx.enter_context(nc.sbuf_tensor(name, shape, dt))

        def sem(name):
            return ctx.enter_context(nc.semaphore(name))

        wqT_sb = sb("wqT_sb", [P, PAIRS, D])
        wo_hi = sb("wo_hi", [P, PAIRS, D], F32R)
        wo_lo = sb("wo_lo", [P, PAIRS, D], F32R)
        kh_all = sb("kh_all", [P, PAIRS, AK])
        bq_blk = sb("bq_blk", [P, PAIRS * HEADS])
        m_all = sb("m_all", [P, DC, (NB - 1) * KEYS + P])
        rb0 = sb("rb0", [P, AK])
        vvs_hi = sb("vvs_hi", [P, NB * BANK], F32R)
        vvs_lo = sb("vvs_lo", [P, NB * BANK], F32R)
        ln_gb = sb("ln_gb", [P, 2, D])
        ident = sb("ident", [P, P])
        cols_sb = sb("cols_sb", [P, NCOLS])
        small = sb("small", [P, 8])
        bk8 = sb("bk8", [P, PAIRS])
        bo_sb = sb("bo_sb", [P, D])
        blk_k = sb("blk_k", [P, PAIRS * PW])
        blk_v_hi = sb("blk_v_hi", [P, VWIDTH], F32R)
        blk_v_lo = sb("blk_v_lo", [P, VWIDTH], F32R)
        g_hi = sb("g_hi", [P, DC, HK], F32R)
        g_lo = sb("g_lo", [P, DC, HK], F32R)
        vo_hi = sb("vo_hi", [P, CH, D], F32R)
        vo_lo = sb("vo_lo", [P, CH, D], F32R)
        rb1 = sb("rb1", [P, HK])
        fs = sb("fs", [P, SLOTS * HKP])
        pt_hi = sb("pt_hi", [P, CH, P], F32R)
        pt_lo = sb("pt_lo", [P, CH, P], F32R)
        x1T_hi = sb("x1T_hi", [P, TILES, D], F32R)
        x1T_lo = sb("x1T_lo", [P, TILES, D], F32R)
        xrow = sb("xrow", [P, TILES * D])
        xT_sb = sb("xT_sb", [P, DC, SEQ])
        attn = sb("attn", [P, TILES * P])
        aT_hi = sb("aT_hi", [P, TILES, P], F32R)
        aT_lo = sb("aT_lo", [P, TILES, P], F32R)
        work = sb("work", [P, (YSLOTS + 4) * D])
        y = work[:, 0:YSLOTS * D].rearrange("p (s d) -> p s d", s=YSLOTS)
        th = work[:, YSLOTS * D:(YSLOTS + 2) * D].rearrange("p (s d) -> p s d", s=2)
        o_sb = work[:, (YSLOTS + 2) * D:(YSLOTS + 4) * D].rearrange("p (s d) -> p s d", s=2)
        negmax = sb("negmax", [P, 2, HEADS])
        sums = sb("sums", [P, 2, HEADS])
        rsum = sb("rsum", [P, 2, HEADS])
        negmax0 = sb("negmax0", [P, TILES])
        sums0 = sb("sums0", [P, TILES])
        rsum0 = sb("rsum0", [P, TILES])
        stats = sb("stats", [P, 6])
        meanvar = sb("meanvar", [P, YSLOTS, 2])
        var_eps = sb("var_eps", [P, YSLOTS])
        rstd = sb("rstd", [P, YSLOTS])

        fs_slots = fs[:, :].rearrange("p (s n) -> p s n", s=SLOTS)
        wk_sb = fs_slots[:, 0:DC, 0:HEADS * DK]
        wv_sb = fs_slots[:, DC:2 * DC, 0:HEADS * DK]
        w123 = xrow[:, 0:3 * DC * D].rearrange("p (w n) -> p w n", w=3)
        wsum = attn[:, 0:DC * D]
        warm = attn[:, DC * D:DC * D + P]
        wk_hi, wk_lo = (t[:, :, 0:HEADS * DK] for t in (g_hi, g_lo))
        wv_hi, wv_lo = (t[:, 0:DC * HEADS * DK // D, :].rearrange("p (c k) n -> p c (k n)", c=DC) for t in (vo_hi, vo_lo))
        cT_hi, cT_lo = (t[:, :, :].rearrange("p i n -> p (i n)")[:, 0:DC * AK].rearrange("p (c n) -> p c n", c=DC) for t in (aT_hi, aT_lo))
        wk0_sb = work[:, 0:DC * D].rearrange("p (c n) -> p c n", c=DC)
        wv0_sb = work[:, DC * D:2 * DC * D].rearrange("p (c n) -> p c n", c=DC)
        wq0_sb = work[:, 2 * DC * D:3 * DC * D].rearrange("p (c n) -> p c n", c=DC)
        vvs_raw = [work[0:KEYS, 3 * DC * D:3 * DC * D + BANK], work[0:KEYS, 0:BANK]]
        kT0 = [xrow[:, 3 * DC * D:3 * DC * D + AK], attn[:, DC * D + P:DC * D + P + AK]]
        vT0 = [blk_k[:, 3 * D:3 * D + AK], rb1[:, DC * AK + DC * P:DC * AK + DC * P + AK]]
        wo_raw = fs_slots[:, 0:DC, 0:HEADS * DK]
        vh_parts = [[(x1T if j < V_FIRST else pt)[:, :, :].rearrange("p c n -> p (c n)")[:, (j % V_FIRST) * AK:(j % V_FIRST + 1) * AK]
                     for j in range(PAIRS)] for x1T, pt in ((x1T_hi, pt_hi), (x1T_lo, pt_lo))]
        rb_all = work[0:HEADS, 2 * DC * D:2 * DC * D + AK]
        cT_sb = rb1[:, 0:DC * AK].rearrange("p (c n) -> p c n", c=DC)
        bias_rows = blk_k[:, 0:3 * D].rearrange("p (r d) -> p r d", r=3)
        bq0_rep = rb1[:, DC * AK:DC * AK + DC * P].rearrange("p (c n) -> p c n", c=DC)

        ps = [ctx.enter_context(nc.psum_tensor(f"bank{i}", [P, BANK], F32)) for i in range(8)]
        S_BANK, T_BANK, O_BANK, E_BANK, X_BANK = ps[0:3], ps[3:5], ps[5], ps[6], ps[7]
        L0_BANK = [E_BANK, X_BANK]
        VO_BANK = [E_BANK, X_BANK, O_BANK]
        GATE_BANK = [E_BANK, X_BANK, S_BANK[1], S_BANK[2]]
        X1T_BANK = [T_BANK[1], O_BANK, S_BANK[0]]
        NG, NX = len(GATE_BANK), len(X1T_BANK)
        X1T_IN_S0 = max(i for i in range(TILES) if i % NX == 2)

        ld_ctx, ld_wk0, ld_wv0, ld_wq0, ld_wk, ld_wv = (sem(f"ld_{n}") for n in ("ctx", "wk0", "wv0", "wq0", "wk", "wv"))
        ld_w123, ld_cols, ld_ident, ld_vec, ld_w1 = (sem(f"ld_{n}") for n in ("w123", "cols", "ident", "vec", "w1"))
        f_loaded = [sem(f"f_loaded{i}") for i in range(SLOTS)]
        xT_loaded = sem("xT_loaded")
        x_loaded = [sem(f"x_loaded{g}") for g in range(len(X_PIECES))]
        out_stored = [sem(f"out_stored{i}") for i in range(YSLOTS)]
        ld_wo, v_stored, v_loaded = (sem(n) for n in ("ld_wo", "v_stored", "v_loaded"))
        vh_hi_ready, wo_hi_ready, wo_lo_ready, bo_ready = (sem(n) for n in ("vh_hi_ready", "wo_hi_ready", "wo_lo_ready", "bo_ready"))
        bo_hi_ready = sem("bo_hi_ready")
        consts_set, wsum_ready, su_filled, su_act, su_dve = (sem(n) for n in ("consts_set", "wsum_ready", "su_filled", "su_act", "su_dve"))
        cT_hi_ready, cT_lo_ready, w_hi_ready, w_lo_ready = (sem(n) for n in ("cT_hi_ready", "cT_lo_ready", "w_hi_ready", "w_lo_ready"))
        vvs_hi_ready, vvs_lo_ready, pads_set, bq_ready, warm_ready = (sem(n) for n in ("vvs_hi_ready", "vvs_lo_ready", "pads_set", "bq_ready", "warm_ready"))
        vvs_chain, pool_chain, rb_stored, rb_loaded = (sem(n) for n in ("vvs_chain", "pool_chain", "rb_stored", "rb_loaded"))
        energy_filled, g_filled, attnT_filled = (sem(n) for n in ("energy_filled", "g_filled", "attnT_filled"))
        l0_filled, x1T_filled, vo_filled = (sem(n) for n in ("l0_filled", "x1T_filled", "vo_filled"))
        scores_filled, pT_filled, out_filled = (sem(n) for n in ("scores_filled", "pT_filled", "out_filled"))
        g_hi_ready, exp0_done, aT_hi_ready = (sem(n) for n in ("g_hi_ready", "exp0_done", "aT_hi_ready"))
        tanh_ready, x1T_hi_ready, vo_hi_ready, pT_hi_ready, exp_done = (sem(n) for n in ("tanh_ready", "x1T_hi_ready", "vo_hi_ready", "pT_hi_ready", "exp_done"))
        blk_k_ready, e_biased, negmax0_ready, rsum0_ready, g_lo_ready = (sem(n) for n in (
            "blk_k_ready", "e_biased", "negmax0_ready", "rsum0_ready", "g_lo_ready"))
        aT_lo_ready, gated, x1T_lo_ready, vo_lo_ready = (sem(n) for n in ("aT_lo_ready", "gated", "x1T_lo_ready", "vo_lo_ready"))
        s_biased, negmax_ready, rsum_ready, pT_lo_ready = (sem(n) for n in ("s_biased", "negmax_ready", "rsum_ready", "pT_lo_ready"))
        negmax_early = sem("negmax_early")
        y_summed, y_stats, y_meanvar, var_ready, y_normed = (sem(n) for n in ("y_summed", "y_stats", "y_meanvar", "var_ready", "y_normed"))
        attn_ready, x1_ready, f_biased, probs_ready = (sem(n) for n in ("attn_ready", "x1_ready", "f_biased", "probs_ready"))
        rstd_ready, y_scaled, y_final = (sem(n) for n in ("rstd_ready", "y_scaled", "y_final"))

        def f_slot(s, a=0, b=HK):
            return fs[:, (s % SLOTS) * HKP + a:(s % SLOTS) * HKP + b]

        SETUP = ([("kT0", i, "act") for i in range(DC)] + [("vT0", i, "dve") for i in range(DC)]
                 + [("m", i, "act") for i in range(DC)] + [("rb0", 0, "dve")] + [("vvs", b, "dve") for b in range(NB)]
                 + [("kh", j, "act") for j in range(PAIRS)]
                 + [("vh", j, "dve") for j in range(2)] + [("rb1", 0, "dve")] + [("vh", j, "dve") for j in range(2, PAIRS)])
        N_SETUP = len(SETUP)
        FILL_OF = {(what, n): i for i, (what, n, _) in enumerate(SETUP)}
        VVS_DONE = FILL_OF["vvs", NB - 1] + 1
        N_PADS_EARLY, N_PADS = 6, 10

        def evacuated(i):
            who = SETUP[i][2]
            return (su_act if who == "act" else su_dve), sum(w == who for _, _, w in SETUP[:i + 1])

        block = ctx.enter_context(nc.Block())

        @block.sync
        def _(sp):
            def load_xT(b):
                sp.dma_start(xT_sb[:, :, :], xT_v[:, :, bass.ds(b * SEQ, SEQ)]).then_inc(xT_loaded, 16)

            def load_x(b, g):
                t0, t1 = X_PIECES[g]
                sp.dma_start(xrow[:, t0 * D:t1 * D].rearrange("p (i d) -> p i d", i=t1 - t0),
                             x_v[:, bass.ds(b, 1), t0:t1, :].rearrange("p b i d -> p (b i) d")).then_inc(x_loaded[g], 16)

            def load_f(b, s):
                sp.dma_start(f_slot(s), f_v[:, bass.ds(b * TILES + s, 1), :].rearrange("p t n -> p (t n)")).then_inc(f_loaded[s % SLOTS], 16)

            def load_rb(b):
                sp.dma_start(rb1[:, :], rb_dram[bass.ds(b, 1), :].rearrange("b n -> (b n)").partition_broadcast(P)).then_inc(rb_loaded, 16)

            def load_v(b):
                for part, blk in enumerate((blk_v_hi, blk_v_lo)):
                    for h in range(2):
                        rows = slice(h * DK, (h + 1) * DK)
                        dst = blk[rows, :].bitcast(F32).rearrange("p (r n) -> p r n", r=PAIRS)[:, :, h * KEYS:(h + 1) * KEYS]
                        src = v_dram[part, rows, :].rearrange("p (r n) -> p r n", r=PAIRS)[:, :, bass.ds(b * KEYS, KEYS)]
                        sp.dma_start(dst, src).then_inc(v_loaded, 16)

            def store(b, s):
                sp.wait_ge(y_final, b * TILES + s + 1)
                sp.dma_start(out_v[:, bass.ds(b * TILES + s, 1), :].rearrange("p t n -> p (t n)"),
                             y[:, s % YSLOTS, :]).then_inc(out_stored[s % YSLOTS], 16)

            def batch(b, first, last):
                if not first:
                    store(b - 1, 4)
                    store(b - 1, 5)
                    sp.wait_ge(y_summed, b * TILES - 1)
                    load_x(b, 1)
                    store(b - 1, 6)
                    sp.wait_ge(y_summed, b * TILES)
                    load_x(b, 2)
                for s in range(TILES):
                    if s >= 2:
                        sp.wait_ge(pT_filled, 3 * (b * TILES + s - 1))
                        if s + 2 < TILES:
                            load_f(b, s + 2)
                        elif not last:
                            load_f(b + 1, s + 2 - TILES)
                    elif s + 2 < TILES:
                        if not first:
                            sp.wait_ge(pT_filled, 3 * (b * TILES + s - 1))
                        load_f(b, s + 2)
                    if s == 1 and not first:
                        store(b - 1, 7)
                    if s == 0 and not last:
                        sp.wait_ge(energy_filled, GROUPS * (b + 1))
                        load_xT(b + 1)
                    if s >= 4:
                        store(b, s - 4)
                    if s == 4 and not last:
                        sp.wait_ge(vo_filled, (b + 1) * VO_FILLS)
                        load_v(b + 1)
                    if s == 7 and not last:
                        sp.wait_ge(f_biased, (b + 1) * TILES)
                        load_rb(b + 1)
                    if s == 6 and not last:
                        sp.wait_ge(y_summed, b * TILES + 4)
                        load_x(b + 1, 0)

            sp.dma_start(cT_sb, cT.rearrange("(c p) n -> p c n", p=P)).then_inc(ld_ctx, 16)
            sp.dma_start(wk0_sb, wk0T.rearrange("(c p) n -> p c n", p=P)).then_inc(ld_wk0, 16)
            sp.dma_start(wv0_sb, wv0T.rearrange("(c p) n -> p c n", p=P)).then_inc(ld_wv0, 16)
            sp.dma_start(wq0_sb, wq0.rearrange("(c p) n -> p c n", p=P)).then_inc(ld_wq0, 16)
            for i, w in enumerate((w1T, w2T, w3T)):
                sp.dma_start(w123[:, i, :].rearrange("p (c n) -> p c n", c=DC), w.rearrange("(c p) n -> p c n", p=P)).then_inc(ld_w123, 16)
            sp.dma_start(wk_sb, wk.rearrange("(c p) n -> p c n", p=P)).then_inc(ld_wk, 16)
            sp.dma_start(wv_sb, wv.rearrange("(c p) n -> p c n", p=P)).then_inc(ld_wv, 16)
            load_xT(0)
            sp.dma_start(wqT_sb[:, :, :], wqT.rearrange("(c p) n -> p c n", p=P)).then_inc(ld_w1, 16)
            sp.wait_ge(w_lo_ready, 2)
            for c in range(DC):
                sp.dma_start(wo_raw[:, c, :].rearrange("p (k n) -> p k n", n=D),
                             wo[c * (HEADS * DK // DC):(c + 1) * (HEADS * DK // DC), :].rearrange("(k p) n -> p k n", p=P)).then_inc(ld_wo, 16)
            sp.wait_ge(wsum_ready, 2)
            sp.wait_ge(su_filled, FILL_OF["rb0", 0] + 1)
            for g in range(len(X_PIECES)):
                load_x(0, g)
            sp.wait_ge(wo_lo_ready, 1)
            load_f(0, 0)
            load_f(0, 1)
            sp.wait_ge(*evacuated(FILL_OF["rb1", 0]))
            sp.dma_start(rb_dram.rearrange("b (h n) -> h b n", h=HEADS), rb_all.rearrange("h (b n) -> h b n", b=NB)).then_inc(rb_stored, 16)
            sp.wait_ge(*evacuated(N_SETUP - 1))
            for part, (x1T, pt) in enumerate(((x1T_hi, pt_hi), (x1T_lo, pt_lo))):
                for buf, p0, p1 in ((x1T, 0, V_FIRST), (pt, V_FIRST, PAIRS)):
                    sp.dma_start(v_dram[part, :, p0 * AK:p1 * AK],
                                 buf[:, :, :].bitcast(F32).rearrange("p c n -> p (c n)")[:, 0:(p1 - p0) * AK]).then_inc(v_stored, 16)
            sp.wait_ge(rb_stored, 16)
            load_rb(0)
            sp.wait_ge(v_stored, 64)
            load_v(0)
            batch(0, True, False)
            with sp.Fori(1, NB - 1) as b:
                batch(b, False, False)
            batch(NB - 1, False, True)
            for s in (4, 5, 6, 7):
                store(NB - 1, s)
            for i in range(YSLOTS):
                sp.wait_ge(out_stored[i], 16 * NB * TILES // YSLOTS)

        @block.tensor
        def _(pe):
            mm = nc.tensor.matmul

            def three_pass(dst, a_hi, a_lo, b_hi, b_lo, start, stop):
                mm(dst, a_hi, b_hi, start=start, stop=False)
                mm(dst, a_hi, b_lo, start=False, stop=False)
                return mm(dst, a_lo, b_hi, start=False, stop=stop)

            def setup():
                pe.wait_ge(warm_ready, 1)
                for _ in range(WARM_UPS):
                    mm(ps[7][:, 0:P], warm, warm, start=True, stop=True)
                pe.wait_ge(ld_ctx, 16)
                loads = {"kT0": (ld_wk0, 16), "vT0": (ld_wv0, 16), "m": (ld_wq0, 16)}
                for i, (what, n, _) in enumerate(SETUP):
                    if i >= 8:
                        pe.wait_ge(*evacuated(i - 8))
                    dst = ps[i % 8]
                    if n == 0 and what in loads:
                        pe.wait_ge(*loads[what])
                    if what in ("kh", "vh"):
                        pe.wait_ge(w_lo_ready, (1 if what == "kh" else 3) + n // (PAIRS // 2))
                    if what == "kh" and n == 0:
                        pe.wait_ge(cT_lo_ready, 1)
                    if what == "m" and n == 0:
                        pe.wait_ge(*evacuated(FILL_OF["kT0", DC - 1]))
                    if what == "rb0":
                        pe.wait_ge(consts_set, 1)
                    if what == "rb1":
                        pe.wait_ge(bq_ready, 1)
                        pe.wait_ge(*evacuated(FILL_OF["kh", PAIRS - 1]))
                        for pr in range(PAIRS):
                            ins = mm(dst[0:HEADS, 0:AK], bq_blk[:, pr * HEADS:(pr + 1) * HEADS], kh_all[:, pr, :], start=pr == 0, stop=pr == PAIRS - 1)
                        ins.then_inc(su_filled, 1)
                        continue
                    if what == "vvs" and n == 0:
                        pe.wait_ge(ld_ident, 16)
                        pe.wait_ge(*evacuated(FILL_OF["vT0", DC - 1]))
                        pe.wait_ge(wsum_ready, 2)
                    for c in range(DC):
                        first, last = c == 0, c == DC - 1
                        if what == "kT0":
                            ins = mm(dst[:, 0:AK], wk0_sb[:, c, n * P:(n + 1) * P], cT_sb[:, c, :], start=first, stop=last)
                        elif what == "vT0":
                            ins = mm(dst[:, 0:AK], wv0_sb[:, c, n * P:(n + 1) * P], cT_sb[:, c, :], start=first, stop=last)
                        elif what == "kh":
                            ins = three_pass(dst[:, 0:AK], wk_hi[:, c, n * P:(n + 1) * P], wk_lo[:, c, n * P:(n + 1) * P],
                                             cT_hi[:, c, :], cT_lo[:, c, :], first, last)
                        elif what == "vh":
                            ins = three_pass(dst[:, 0:AK], wv_hi[:, c, n * P:(n + 1) * P], wv_lo[:, c, n * P:(n + 1) * P],
                                             cT_hi[:, c, :], cT_lo[:, c, :], first, last)
                        elif what == "m":
                            ins = mm(dst[:, 0:AK], wq0_sb[:, c, n * P:(n + 1) * P], kT0[c], start=first, stop=last)
                        elif what == "rb0":
                            ins = mm(dst[:, 0:AK], bq0_rep[:, c, :], kT0[c], start=first, stop=last)
                        elif what == "vvs":
                            ins = nc.tensor.transpose(dst[0:KEYS, c * P:(c + 1) * P], vT0[c][:, n * KEYS:(n + 1) * KEYS], ident[:, :])
                    if what == "vvs":
                        for c in range(DC):
                            ins = mm(dst[0:KEYS, D:2 * D], vT0[c][:, n * KEYS:(n + 1) * KEYS], wsum[:, c * D:(c + 1) * D],
                                     start=c == 0, stop=c == DC - 1)
                    ins.then_inc(su_filled, 1)

            def energy(b, g, prev):
                if prev:
                    pe.wait_ge(vo_lo_ready, b * VO_FILLS)
                for i in range(GROUP):
                    for c in range(DC):
                        ins = mm(L0_BANK[g][:, i * P:(i + 1) * P], xT_sb[:, c, (g * GROUP + i) * P:(g * GROUP + i + 1) * P],
                                 m_all[:, c, bass.ds(b * KEYS, P)], start=c == 0, stop=c == DC - 1)
                ins.then_inc(energy_filled, 1)

            def g_fill(b, n, prev):
                c, k = n // 3, n % 3
                if c == 0 and prev:
                    pe.wait_ge(s_biased, 3 * b * TILES - 2 + k)
                elif c:
                    pe.wait_ge(g_lo_ready, b * 6 + n - 2)
                a, e = SCORE_PAIRS[k]
                for pr in range(a, e):
                    ins = mm(S_BANK[k][:, (pr - a) * PW:(pr - a + 1) * PW], wqT_sb[:, pr, c * P:(c + 1) * P],
                             blk_k[:, pr * PW:(pr + 1) * PW], start=True, stop=True)
                ins.then_inc(g_filled, 1)

            def attnT(b, g):
                pe.wait_ge(e_biased, b * GROUPS + g + 1)
                pe.wait_ge(attn_ready, b * GROUPS + g + 1)
                for i in range(GROUP):
                    ins = nc.tensor.transpose(L0_BANK[g][:, i * P:(i + 1) * P], attn[:, (g * GROUP + i) * P:(g * GROUP + i + 1) * P], ident[:, :])
                ins.then_inc(attnT_filled, 1)

            def l0_out(b, i):
                if i % GROUP == 0:
                    pe.wait_ge(aT_lo_ready, b * GROUPS + i // GROUP + 1)
                if i == 1:
                    pe.wait_ge(aT_lo_ready, b * GROUPS + 2)
                elif i in (2, 3):
                    pe.wait_ge(g_lo_ready, b * 6 + 3 + i)
                elif i >= NG:
                    pe.wait_ge(gated, b * TILES + i - NG + 1)
                v = bass.ds(b * BANK, BANK)
                three_pass(GATE_BANK[i % NG][:, :], aT_hi[:, i, :], aT_lo[:, i, :], vvs_hi[:, v], vvs_lo[:, v], True, True).then_inc(l0_filled, 1)

            def x1T(b, i, prev):
                pe.wait_ge(x1_ready, b * TILES + i + 1)
                if i >= NX:
                    pe.wait_ge(x1T_lo_ready, b * TILES + i - NX + 1)
                elif i == 2:
                    pe.wait_ge(g_lo_ready, b * 6 + 4)
                elif prev and i == 1:
                    pe.wait_ge(y_summed, b * TILES)
                elif prev:
                    pe.wait_ge(pT_lo_ready, 3 * b * TILES - 1)
                for c in range(DC):
                    ins = nc.tensor.transpose(X1T_BANK[i % NX][:, c * P:(c + 1) * P], xrow[:, i * D + c * P:i * D + (c + 1) * P], ident[:, :])
                ins.then_inc(x1T_filled, 1)

            def vo_fill(b, n, prev):
                if n == 0:
                    pe.wait_ge(v_loaded, 64 * (b + 1))
                    if not prev:
                        pe.wait_ge(wo_lo_ready, 1)
                        pe.wait_ge(bo_ready, 2)
                if n < 2:
                    pe.wait_ge(gated, b * TILES + TILES - NG + n + 1)
                elif n == 2:
                    pe.wait_ge(x1T_lo_ready, (b + 1) * TILES)
                else:
                    pe.wait_ge(vo_lo_ready, b * VO_FILLS + n - 2)
                for half in range(2):
                    c = 2 * n + half
                    dst = VO_BANK[n % len(VO_BANK)][:, half * D:(half + 1) * D]
                    pairs = [pr for pr in range(PAIRS) if pr * PW < (c + 1) * P and (pr + 1) * PW > c * P]
                    for pr in pairs:
                        at = pr * VSTRIDE + c * P - pr * PW
                        ins = three_pass(dst, blk_v_hi[:, at:at + P], blk_v_lo[:, at:at + P], wo_hi[:, pr, :], wo_lo[:, pr, :],
                                         pr == pairs[0], pr == pairs[-1])
                ins.then_inc(vo_filled, 1)

            def scores(b, s, k, first_tile_of_batch):
                if k == 0:
                    pe.wait_ge(x1T_lo_ready, b * TILES + s + 1)
                if first_tile_of_batch:
                    if k == 0:
                        pe.wait_ge(g_lo_ready, (b + 1) * 6)
                        pe.wait_ge(x1T_lo_ready, b * TILES + X1T_IN_S0 + 1)
                    else:
                        pe.wait_ge(gated, (b + 1) * TILES)
                else:
                    pe.wait_ge(s_biased, 3 * (b * TILES + s) - 2 + k)
                a, e = SCORE_COLS[k]
                for c in range(DC):
                    ins = three_pass(S_BANK[k][:, 0:e - a], x1T_hi[:, s, c * P:(c + 1) * P], x1T_lo[:, s, c * P:(c + 1) * P],
                                     g_hi[:, c, a:e], g_lo[:, c, a:e], c == 0, c == DC - 1)
                ins.then_inc(scores_filled, 1)

            def pT(b, s, k, prev=True):
                at = 3 * (b * TILES + s)
                if k < 2:
                    pe.wait_ge(probs_ready, 2 * (b * TILES + s) + k + 1)
                if k == 2:
                    pe.wait_ge(pT_lo_ready, at + 1)
                elif s == 0 and k == 1:
                    pe.wait_ge(x1T_lo_ready, (b + 1) * TILES)
                elif prev or s > 0:
                    pe.wait_ge(pT_lo_ready, at - (0 if k == 0 else 1))
                c0, c1 = PT_FILLS[k]
                for c in range(c0, c1):
                    ins = nc.tensor.transpose(T_BANK[PT_BANK[k]][:, (c - c0) * P:(c - c0 + 1) * P],
                                              f_slot(s, c * P, (c + 1) * P), ident[:, :])
                ins.then_inc(pT_filled, 1)

            def pv(b, s, k):
                pe.wait_ge(pT_lo_ready, 3 * (b * TILES + s) + k + 1)
                if k == 0 and s == 0:
                    pe.wait_ge(vo_lo_ready, (b + 1) * VO_FILLS)
                elif k == 0:
                    pe.wait_ge(y_summed, b * TILES + s)
                c0, c1 = PT_FILLS[k]
                for c in range(c0, c1):
                    ins = three_pass(O_BANK[:, 0:D], pt_hi[:, c, :], pt_lo[:, c, :], vo_hi[:, c, :], vo_lo[:, c, :], c == 0, c == CH - 1)
                if k == 2:
                    ins.then_inc(out_filled, 1)

            def head(b, prev, cur):
                if cur:
                    pe.wait_ge(xT_loaded, 16 * (b + 1))
                    energy(b, 0, prev)
                    energy(b, 1, prev)
                if prev:
                    pT(b - 1, 6, 0)
                    pT(b - 1, 6, 1)
                if cur:
                    pe.wait_ge(blk_k_ready, b + 1)
                    for n in range(3):
                        g_fill(b, n, prev)
                if prev:
                    pT(b - 1, 6, 2)
                    pv(b - 1, 6, 0)
                if cur:
                    attnT(b, 0)
                if cur:
                    for n in range(3, 6):
                        g_fill(b, n, prev)
                    attnT(b, 1)
                if prev:
                    pv(b - 1, 6, 1)
                    pv(b - 1, 6, 2)
                    pT(b - 1, 7, 0)
                if cur:
                    l0_out(b, 0)
                    l0_out(b, 1)
                    l0_out(b, 2)
                if prev:
                    pT(b - 1, 7, 1)
                    pT(b - 1, 7, 2)
                    pv(b - 1, 7, 0)
                if cur:
                    l0_out(b, 3)
                if prev:
                    pv(b - 1, 7, 1)
                    pv(b - 1, 7, 2)
                if cur:
                    for i in range(L0_EARLY, TILES):
                        l0_out(b, i)
                        for j in X1T_AFTER[i]:
                            x1T(b, j, prev)
                    vo_fill(b, 0, prev)
                    x1T(b, X1T_LATE[0], prev)

            def batch(b, prev):
                head(b, prev, True)
                for s in range(TILES):
                    if s == 0:
                        scores(b, 0, 0, True)
                        x1T(b, X1T_LATE[1], prev)
                        scores(b, 0, 1, True)
                        scores(b, 0, 2, True)
                        vo_fill(b, 1, prev)
                        continue
                    if s == 1:
                        for k in range(3):
                            scores(b, 1, k, False)
                        for n in (2, 3, 4):
                            vo_fill(b, n, prev)
                        continue
                    pT(b, s - 2, 0, prev)
                    scores(b, s, 0, False)
                    pT(b, s - 2, 1)
                    scores(b, s, 1, False)
                    pT(b, s - 2, 2)
                    pv(b, s - 2, 0)
                    scores(b, s, 2, False)
                    pv(b, s - 2, 1)
                    pv(b, s - 2, 2)

            setup()
            pe.wait_ge(*evacuated(N_SETUP - 8 + 3))
            pe.wait_ge(pads_set, N_PADS)
            pe.wait_ge(ld_w1, 16)
            batch(0, False)
            with pe.Fori(1, NB) as b:
                batch(b, True)
            head(NB, True, False)

        @block.scalar
        def _(act):
            copy = nc.scalar.copy
            act.dma_start(cols_sb[:, :], cols).then_inc(ld_cols, 16)
            act.dma_start(ident[:, :], ident_in).then_inc(ld_ident, 16)
            act.dma_start(small[:, 0:1], gamma.partition_broadcast(P)).then_inc(ld_vec, 16)
            act.dma_start(bias_rows, rows[R_B1:R_B3 + 1, :].partition_broadcast(P)).then_inc(ld_vec, 16)
            act.dma_start(bo_sb[ONE_ROW:ONE_ROW + 1, :], bo).then_inc(ld_vec, 16)
            act.dma_start(ln_gb[:, :, :], rows[R_LNG:R_LNB + 1, :].partition_broadcast(P)).then_inc(ld_vec, 16)

            def setup():
                act.wait_ge(ld_cols, 16)
                for c in range(DC):
                    ins = copy(bq0_rep[:, c, :], cols_sb[:, C_BQ0 + c:C_BQ0 + c + 1].broadcast_to([P, P]))
                ins.then_inc(consts_set, 1)
                act.wait_ge(pads_set, N_PADS_EARLY)
                for i, (what, n, who) in enumerate(SETUP):
                    src = ps[i % 8][:, 0:AK]
                    if what == "vvs":
                        act.wait_ge(*evacuated(i))
                        copy(vvs_hi[0:KEYS, n * BANK:(n + 1) * BANK], vvs_raw[n % 2]).then_inc(vvs_hi_ready, 1)
                        continue
                    if what == "vh":
                        if n == 0:
                            act.wait_ge(ld_wo, 16 * DC)
                            copy(wo_hi[:, :, :].rearrange("p (c k) n -> p c (k n)", c=DC), wo_raw).then_inc(wo_hi_ready, 1)
                        act.wait_ge(su_filled, i + 1)
                        nc.scalar.activation(vh_parts[0][n], src, ACT.Identity, bias=cols_sb[:, C_BV1 + n:C_BV1 + n + 1]).then_inc(vh_hi_ready, 1)
                        continue
                    if who != "act":
                        if what == "rb0":
                            copy(cT_hi, cT_sb).then_inc(cT_hi_ready, 1)
                            for loaded, raw, hi in ((ld_wk, wk_sb, wk_hi), (ld_wv, wv_sb, wv_hi)):
                                act.wait_ge(loaded, 16)
                                for a, e in W_HALVES:
                                    copy(hi[:, :, a:e], raw[:, :, a:e]).then_inc(w_hi_ready, 1)
                        continue
                    act.wait_ge(su_filled, i + 1)
                    if what == "kT0":
                        ins = nc.scalar.activation(kT0[n], src, ACT.Identity, bias=cols_sb[:, C_BK0 + n:C_BK0 + n + 1])
                    elif what == "kh":
                        if n == 0:
                            act.wait_ge(wsum_ready, 1)
                        ins = nc.scalar.activation(kh_all[:, n, :], src, ACT.Identity, bias=bk8[:, n:n + 1], scale=SCALE)
                    else:
                        ins = copy(m_all[:, n, 0:AK], src)
                    ins.then_inc(su_act, 1)

            def g_split(b, n):
                c, k = n // 3, n % 3
                a, e = SCORE_COLS[k]
                act.wait_ge(g_filled, b * 6 + n + 1)
                copy(g_hi[:, c, a:e], S_BANK[k][:, 0:e - a]).then_inc(g_hi_ready, 1)

            def vo_split(b, n):
                act.wait_ge(vo_filled, b * VO_FILLS + n + 1)
                if n < VO_FILLS - 1:
                    copy(vo_hi[:, 2 * n:2 * n + 2, :].rearrange("p c n -> p (c n)"), VO_BANK[n % len(VO_BANK)][:, :]).then_inc(vo_hi_ready, 1)
                else:
                    copy(vo_hi[:, 2 * n, :], VO_BANK[n % len(VO_BANK)][:, 0:D])
                    copy(vo_hi[0:ONE_ROW, 2 * n + 1, :], VO_BANK[n % len(VO_BANK)][0:ONE_ROW, D:2 * D]).then_inc(vo_hi_ready, 1)

            def bo_row():
                act.wait_ge(bo_ready, 1)
                act.wait_ge(ld_vec, 64)
                copy(vo_hi[ONE_ROW:ONE_ROW + 1, CH - 1, :], bo_sb[ONE_ROW:ONE_ROW + 1, :]).then_inc(bo_hi_ready, 1)

            def exp0(b, g):
                act.wait_ge(negmax0_ready, b * GROUPS + g + 1)
                for i in range(g * GROUP, (g + 1) * GROUP):
                    e = attn[:, i * P:i * P + KEYS]
                    ins = nc.scalar.activation(e, e, ACT.Exp, bias=negmax0[:, i:i + 1], accum_out=sums0[:, i:i + 1])
                ins.then_inc(exp0_done, 1)

            def aT_split(b, g):
                act.wait_ge(attnT_filled, b * GROUPS + g + 1)
                copy(aT_hi[:, g * GROUP:(g + 1) * GROUP, :].rearrange("p i n -> p (i n)"), L0_BANK[g][:, :]).then_inc(aT_hi_ready, 1)

            def tanh(b, i):
                act.wait_ge(l0_filled, b * TILES + i + 1)
                if i >= 2:
                    act.wait_ge(gated, b * TILES + i - 1)
                nc.scalar.activation(th[:, i % 2, :], GATE_BANK[i % NG][:, D:2 * D], ACT.Tanh, scale=0.5).then_inc(tanh_ready, 1)

            def x1T_split(b, i):
                act.wait_ge(x1T_filled, b * TILES + i + 1)
                copy(x1T_hi[:, i, :], X1T_BANK[i % NX][:, 0:D]).then_inc(x1T_hi_ready, 1)

            def pT_split(b, s, k):
                c0, c1 = PT_FILLS[k]
                act.wait_ge(pT_filled, 3 * (b * TILES + s) + k + 1)
                copy(pt_hi[:, c0:c1, :].rearrange("p c n -> p (c n)"), T_BANK[PT_BANK[k]][:, 0:(c1 - c0) * P]).then_inc(pT_hi_ready, 1)

            def exp(b, s, h0, h1):
                if s == 0 and h0 == 0:
                    act.wait_ge(negmax_early, b + 1)
                elif h0 == 0:
                    act.wait_ge(negmax_ready, b * TILES + s + 1)
                for h in range(h0, h1):
                    if s == 0 and h == EARLY_HEADS:
                        act.wait_ge(negmax_ready, b * TILES + 1)
                    e = f_slot(s, h * KEYS, (h + 1) * KEYS)
                    ins = nc.scalar.activation(e, e, ACT.Exp, bias=negmax[:, s % 2, h:h + 1], accum_out=sums[:, s % 2, h:h + 1])
                    if h + 1 in (HALVES[0][1], HALVES[1][1]):
                        ins.then_inc(exp_done, 1)

            def head(b, prev, cur):
                if prev and cur:
                    exp(b - 1, 7, 0, 8)
                    exp0(b, 0)
                    pT_split(b - 1, 6, 0)
                    pT_split(b - 1, 6, 1)
                elif prev:
                    exp(b - 1, 7, 0, 8)
                else:
                    exp0(b, 0)
                if cur:
                    for n in range(3):
                        g_split(b, n)
                if prev and cur:
                    pT_split(b - 1, 6, 2)
                if cur:
                    exp0(b, 1)
                    aT_split(b, 0)
                for n in range(3, 6):
                    if prev:
                        exp(b - 1, 7, *EXP7_SPLIT[n - 3:n - 1])
                    if cur:
                        g_split(b, n)
                if cur:
                    aT_split(b, 1)
                if prev:
                    exp(b - 1, 7, EXP7_SPLIT[3], HEADS)
                    pT_split(b - 1, 7, 0)
                if cur:
                    if not prev:
                        bo_row()
                        act.wait_ge(v_stored, 64)
                        act.wait_ge(rb_stored, 16)
                    tanh(b, 0)
                    tanh(b, 1)
                if prev:
                    pT_split(b - 1, 7, 1)
                    pT_split(b - 1, 7, 2)
                if cur:
                    tanh(b, 2)
                    tanh(b, 3)
                    for i in range(L0_EARLY, TILES):
                        tanh(b, i)
                        for j in X1T_AFTER[i]:
                            x1T_split(b, j)
                    vo_split(b, 0)
                    for j in X1T_LATE:
                        x1T_split(b, j)

            def batch(b, prev):
                head(b, prev, True)
                for s in range(TILES):
                    if s == 0:
                        exp(b, 0, 0, 3)
                        vo_split(b, 1)
                        exp(b, 0, 3, 13)
                        vo_split(b, 2)
                        exp(b, 0, 13, HEADS)
                        vo_split(b, 3)
                        vo_split(b, 4)
                        exp(b, 1, 0, 2)
                        continue
                    if s == 1:
                        continue
                    parts = [2, 3, 5, 8, HEADS] if s == 2 else [0, 2, 5, 8, HEADS]
                    for k in range(3):
                        exp(b, s - 1, *parts[k:k + 2])
                        pT_split(b, s - 2, k)
                    exp(b, s - 1, *parts[3:])

            setup()
            act.wait_ge(vvs_lo_ready, NB)
            act.wait_ge(pads_set, N_PADS)
            batch(0, False)
            with act.Fori(1, NB) as b:
                batch(b, True)
            head(NB, True, False)

        @block.vector
        def _(dve):
            v = nc.vector

            def setup():
                dve.wait_ge(ld_cols, 16)
                v.tensor_scalar(bk8[:, :], cols_sb[:, C_BK1:C_BK1 + PAIRS], SCALE, None, ALU.mult).then_inc(wsum_ready, 1)
                for part in (vo_hi, vo_lo):
                    ins = v.memset(part[ONE_ROW:P, CH - 1, :].bitcast(F32), 0.0)
                ins.then_inc(bo_ready, 1)
                dve.wait_ge(pads_set, 1)
                v.tensor_copy(bq_blk[0:DK, 0:P:HEADS + 2], cols_sb[0:DK, C_BQ1:C_BQ1 + PAIRS])
                v.tensor_copy(bq_blk[DK:P, 1:P:HEADS + 2], cols_sb[DK:P, C_BQ1:C_BQ1 + PAIRS]).then_inc(bq_ready, 1)
                for i, (what, n, who) in enumerate(SETUP):
                    if who != "dve":
                        continue
                    if what == "rb0":
                        sums_of_weights()
                        dve.wait_ge(cT_hi_ready, 1)
                        v.tensor_tensor(cT_lo, cT_sb, cT_hi, ALU.subtract).then_inc(cT_lo_ready, 1)
                    src = ps[i % 8][:, 0:AK]
                    dve.wait_ge(su_filled, i + 1)
                    if what == "vT0":
                        ins = v.tensor_scalar(vT0[n], src, cols_sb[:, C_BV0 + n:C_BV0 + n + 1], None, ALU.add)
                    elif what == "vh":
                        dve.wait_ge(vh_hi_ready, n + 1)
                        ins = v.scalar_tensor_tensor(out=vh_parts[1][n], in0=src, scalar=cols_sb[:, C_BV1 + n:C_BV1 + n + 1],
                                                     in1=vh_parts[0][n], op0=ALU.add, op1=ALU.subtract)
                    elif what == "rb0":
                        ins = v.tensor_copy(rb0[:, :], src)
                    elif what == "rb1":
                        ins = v.tensor_scalar(rb_all, ps[i % 8][0:HEADS, 0:AK], 0.5, None, ALU.mult)
                    else:
                        if n >= 2:
                            dve.wait_ge(vvs_lo_ready, n - 1)
                        v.tensor_scalar(vvs_raw[n % 2][:, 0:D], ps[i % 8][0:KEYS, 0:D], small[0:KEYS, 0:1], None, ALU.mult).then_inc(vvs_chain, 1)
                        v.tensor_tensor(vvs_raw[n % 2][:, D:2 * D], ps[i % 8][0:KEYS, D:2 * D], bias_rows[0:KEYS, 0, :],
                                        ALU.add).then_inc(su_dve, 1)
                        if n:
                            vvs_split(n - 1)
                        if n == NB - 1:
                            vvs_split(n)
                        continue
                    ins.then_inc(su_dve, 1)

            def sums_of_weights():
                dve.wait_ge(ld_w123, 48)
                v.tensor_tensor(wsum, w123[:, 0, :], w123[:, 1, :], ALU.add).then_inc(vvs_chain, 1)
                dve.wait_ge(vvs_chain, 1)
                v.tensor_tensor(wsum, wsum, w123[:, 2, :], ALU.add).then_inc(wsum_ready, 1)
                dve.wait_ge(ld_vec, 64)
                v.tensor_scalar(small[:, 0:1], small[:, 0:1], 0.5, None, ALU.mult).then_inc(vvs_chain, 1)
                v.tensor_tensor(bias_rows[:, 0, :], bias_rows[:, 0, :], bias_rows[:, 1, :], ALU.add).then_inc(vvs_chain, 1)
                dve.wait_ge(vvs_chain, 3)
                v.tensor_tensor(bias_rows[:, 0, :], bias_rows[:, 0, :], bias_rows[:, 2, :], ALU.add).then_inc(vvs_chain, 1)
                dve.wait_ge(vvs_chain, 4)
                dve.wait_ge(pads_set, N_PADS_EARLY)

            def vvs_split(n):
                dve.wait_ge(vvs_hi_ready, n + 1)
                v.tensor_tensor(vvs_lo[0:KEYS, n * BANK:(n + 1) * BANK], vvs_raw[n % 2],
                                vvs_hi[0:KEYS, n * BANK:(n + 1) * BANK], ALU.subtract).then_inc(vvs_lo_ready, 1)

            def blk_k_copy(b, prev):
                if prev:
                    dve.wait_ge(g_filled, 6 * b)
                view = blk_k[:, :].rearrange("p (r n) -> p r n", r=PAIRS)
                v.tensor_copy(view[0:DK, :, 0:KEYS], kh_all[0:DK, :, bass.ds(b * KEYS, KEYS)])
                v.tensor_copy(view[DK:P, :, KEYS:PW], kh_all[DK:P, :, bass.ds(b * KEYS, KEYS)]).then_inc(blk_k_ready, 1)

            def energy(b, g):
                e = attn[:, g * GROUP * P:(g + 1) * GROUP * P].rearrange("p (i n) -> p i n", i=GROUP)[:, :, 0:KEYS]
                dve.wait_ge(energy_filled, b * GROUPS + g + 1)
                v.tensor_tensor(e, L0_BANK[g][:, :].rearrange("p (i n) -> p i n", i=GROUP)[:, :, 0:KEYS],
                                rb0[:, bass.ds(b * KEYS, KEYS)].unsqueeze(1).broadcast_to([P, GROUP, KEYS]), ALU.add).then_inc(e_biased, 1)
                dve.wait_ge(e_biased, b * GROUPS + g + 1)
                v.tensor_reduce(negmax0[:, g * GROUP:(g + 1) * GROUP], e, AX.X, ALU.max, negate=True).then_inc(negmax0_ready, 1)

            def rsum0_of(b, g):
                dve.wait_ge(exp0_done, b * GROUPS + g + 1)
                v.reciprocal(rsum0[:, g * GROUP:(g + 1) * GROUP], sums0[:, g * GROUP:(g + 1) * GROUP]).then_inc(rsum0_ready, 1)

            def g_split(b, n):
                c, k = n // 3, n % 3
                a, e = SCORE_COLS[k]
                dve.wait_ge(g_hi_ready, b * 6 + n + 1)
                v.tensor_tensor(g_lo[:, c, a:e], S_BANK[k][:, 0:e - a], g_hi[:, c, a:e], ALU.subtract).then_inc(g_lo_ready, 1)

            def aT_split(b, g):
                dve.wait_ge(aT_hi_ready, b * GROUPS + g + 1)
                sl = slice(g * GROUP, (g + 1) * GROUP)
                v.tensor_tensor(aT_lo[:, sl, :].rearrange("p i n -> p (i n)"), L0_BANK[g][:, :],
                                aT_hi[:, sl, :].rearrange("p i n -> p (i n)"), ALU.subtract).then_inc(aT_lo_ready, 1)

            def gate(b, i, prev):
                dve.wait_ge(tanh_ready, b * TILES + i + 1)
                if i >= 2 or prev:
                    dve.wait_ge(x1_ready, b * TILES + i - 1)
                v.scalar_tensor_tensor(out=o_sb[:, i % 2, :], in0=th[:, i % 2, :], scalar=1.0, in1=GATE_BANK[i % NG][:, 0:D],
                                       op0=ALU.add, op1=ALU.mult).then_inc(gated, 1)

            def x1T_split(b, i):
                dve.wait_ge(x1T_hi_ready, b * TILES + i + 1)
                v.tensor_tensor(x1T_lo[:, i, :], X1T_BANK[i % NX][:, 0:D], x1T_hi[:, i, :], ALU.subtract).then_inc(x1T_lo_ready, 1)

            def vo_split(b, n):
                dve.wait_ge(vo_hi_ready, b * VO_FILLS + n + 1)
                if n < VO_FILLS - 1:
                    v.tensor_tensor(vo_lo[:, 2 * n:2 * n + 2, :].rearrange("p c n -> p (c n)"), VO_BANK[n % len(VO_BANK)][:, :],
                                    vo_hi[:, 2 * n:2 * n + 2, :].rearrange("p c n -> p (c n)"), ALU.subtract).then_inc(vo_lo_ready, 1)
                else:
                    v.tensor_tensor(vo_lo[:, 2 * n, :], VO_BANK[n % len(VO_BANK)][:, 0:D], vo_hi[:, 2 * n, :], ALU.subtract)
                    v.tensor_tensor(vo_lo[0:ONE_ROW, 2 * n + 1, :], VO_BANK[n % len(VO_BANK)][0:ONE_ROW, D:2 * D],
                                    vo_hi[0:ONE_ROW, 2 * n + 1, :], ALU.subtract).then_inc(vo_lo_ready, 1)

            def s_bias(b, s, k):
                a, e = SCORE_COLS[k]
                if k == 0:
                    dve.wait_ge(f_biased, b * TILES + s + 1)
                dve.wait_ge(scores_filled, 3 * (b * TILES + s) + k + 1)
                v.scalar_tensor_tensor(out=f_slot(s, a, e), in0=f_slot(s, a, e), scalar=2.0, in1=S_BANK[k][:, 0:e - a],
                                       op0=ALU.mult, op1=ALU.add).then_inc(s_biased, 1)

            def s_max(b, s, h0=0):
                dve.wait_ge(s_biased, 3 * (b * TILES + s + 1))
                v.tensor_reduce(negmax[:, s % 2, h0:HEADS], f_slot(s, h0 * KEYS, HK).rearrange("p (h n) -> p h n", n=KEYS), AX.X, ALU.max,
                                negate=True).then_inc(negmax_ready, 1)

            def s_max_early(b):
                dve.wait_ge(s_biased, 3 * b * TILES + 1)
                v.tensor_reduce(negmax[:, 0, 0:EARLY_HEADS], f_slot(0, 0, EARLY_HEADS * KEYS).rearrange("p (h n) -> p h n", n=KEYS), AX.X, ALU.max,
                                negate=True).then_inc(negmax_early, 1)

            def recip(b, s, half):
                h0, h1 = HALVES[half]
                dve.wait_ge(exp_done, 2 * (b * TILES + s) + half + 1)
                v.reciprocal(rsum[:, s % 2, h0:h1], sums[:, s % 2, h0:h1]).then_inc(rsum_ready, 1)

            def pT_copy(b, s, k):
                c0, c1 = PT_FILLS[k]
                dve.wait_ge(pT_filled, 3 * (b * TILES + s) + k + 1)
                v.tensor_copy(pt_hi[:, c0:c1, :].rearrange("p c n -> p (c n)"), T_BANK[PT_BANK[k]][:, 0:(c1 - c0) * P]).then_inc(pT_hi_ready, 1)

            def pT_split(b, s, k):
                c0, c1 = PT_FILLS[k]
                dve.wait_ge(pT_hi_ready, 3 * (b * TILES + s) + k + 1)
                v.tensor_tensor(pt_lo[:, c0:c1, :].rearrange("p c n -> p (c n)"), T_BANK[PT_BANK[k]][:, 0:(c1 - c0) * P],
                                pt_hi[:, c0:c1, :].rearrange("p c n -> p (c n)"), ALU.subtract).then_inc(pT_lo_ready, 1)

            def ln_stats(b, s, may_be_first):
                t = b * TILES + s
                if not (may_be_first and s < YSLOTS):
                    dve.wait_ge(out_stored[s % YSLOTS], 16 * (TILES // YSLOTS) * b + 16 * (s // YSLOTS))
                dve.wait_ge(out_filled, t + 1)
                yt = y[:, s % YSLOTS, :]
                v.tensor_tensor(yt, O_BANK[:, 0:D], xrow[:, s * D:(s + 1) * D], ALU.add).then_inc(y_summed, 1)
                dve.wait_ge(y_summed, t + 1)
                v.bn_stats(stats[:, :], yt).then_inc(y_stats, 1)
                dve.wait_ge(ld_vec, 64)
                dve.wait_ge(y_stats, t + 1)
                v.bn_aggr(meanvar[:, s % YSLOTS, :], stats[:, :]).then_inc(y_meanvar, 1)
                dve.wait_ge(y_meanvar, t + 1)
                v.tensor_scalar(var_eps[:, s % YSLOTS:s % YSLOTS + 1], meanvar[:, s % YSLOTS, 1:2], EPS, None, ALU.add).then_inc(var_ready, 1)

            def ln_norm(b, s):
                yt = y[:, s % YSLOTS, :]
                dve.wait_ge(rstd_ready, b * TILES + s + 1)
                v.tensor_scalar(yt, yt, meanvar[:, s % YSLOTS, 0:1], rstd[:, s % YSLOTS:s % YSLOTS + 1],
                                ALU.subtract, ALU.mult).then_inc(y_normed, 1)

            def ln_affine_last(b):
                yt = y[:, (TILES - 1) % YSLOTS, :]
                dve.wait_ge(y_normed, (b + 1) * TILES)
                v.tensor_tensor(yt, yt, ln_gb[:, 0, :], ALU.mult).then_inc(y_scaled, 1)
                dve.wait_ge(y_scaled, (b + 1) * TILES)
                v.tensor_tensor(yt, yt, ln_gb[:, 1, :], ALU.add).then_inc(y_final, 1)

            def head(b, prev, cur):
                if cur:
                    blk_k_copy(b, prev)
                    energy(b, 0)
                    energy(b, 1)
                if prev:
                    if not cur:
                        pT_copy(b - 1, 6, 0)
                    pT_split(b - 1, 6, 0)
                if cur:
                    rsum0_of(b, 0)
                if prev:
                    if not cur:
                        pT_copy(b - 1, 6, 1)
                        pT_split(b - 1, 6, 1)
                        recip(b - 1, 7, 0)
                        pT_copy(b - 1, 6, 2)
                    else:
                        recip(b - 1, 7, 0)
                        pT_split(b - 1, 6, 1)
                if cur:
                    for n in range(3):
                        g_split(b, n)
                if prev:
                    pT_split(b - 1, 6, 2)
                    ln_norm(b - 1, 5)
                if cur:
                    rsum0_of(b, 1)
                    aT_split(b, 0)
                    for n in range(3, 6):
                        g_split(b, n)
                    aT_split(b, 1)
                if prev:
                    recip(b - 1, 7, 1)
                    pT_split(b - 1, 7, 0)
                    ln_stats(b - 1, 6, False)
                if cur:
                    if not prev:
                        dve.wait_ge(bo_hi_ready, 1)
                        dve.wait_ge(ld_vec, 64)
                        v.tensor_tensor(vo_lo[ONE_ROW:ONE_ROW + 1, CH - 1, :], bo_sb[ONE_ROW:ONE_ROW + 1, :],
                                        vo_hi[ONE_ROW:ONE_ROW + 1, CH - 1, :], ALU.subtract).then_inc(bo_ready, 1)
                        dve.wait_ge(v_stored, 64)
                    gate(b, 0, prev)
                    gate(b, 1, prev)
                if prev:
                    pT_split(b - 1, 7, 1)
                    pT_split(b - 1, 7, 2)
                    ln_norm(b - 1, 6)
                if cur:
                    gate(b, 2, prev)
                    gate(b, 3, prev)
                if prev:
                    ln_stats(b - 1, 7, False)
                if cur:
                    for i in range(L0_EARLY, TILES):
                        gate(b, i, prev)
                        for j in X1T_AFTER[i]:
                            x1T_split(b, j)
                    vo_split(b, 0)
                    x1T_split(b, X1T_LATE[0])
                elif prev:
                    ln_norm(b - 1, 7)
                    ln_affine_last(b - 1)

            def batch(b, prev):
                head(b, prev, True)
                for s in range(TILES):
                    if s < 2:
                        if s == 0:
                            s_bias(b, 0, 0)
                            s_max_early(b)
                            x1T_split(b, X1T_LATE[1])
                            s_bias(b, 0, 1)
                            s_bias(b, 0, 2)
                            s_max(b, 0, EARLY_HEADS)
                            if prev:
                                ln_norm(b - 1, 7)
                            vo_split(b, 1)
                        else:
                            s_bias(b, 1, 0)
                            s_bias(b, 1, 1)
                            recip(b, 0, 0)
                            s_bias(b, 1, 2)
                            s_max(b, 1)
                            vo_split(b, 2)
                            recip(b, 0, 1)
                            vo_split(b, 3)
                            vo_split(b, 4)
                        continue
                    pT_split(b, s - 2, 0)
                    s_bias(b, s, 0)
                    pT_split(b, s - 2, 1)
                    if s > 2:
                        ln_norm(b, s - 3)
                    s_bias(b, s, 1)
                    pT_split(b, s - 2, 2)
                    recip(b, s - 1, 0)
                    s_bias(b, s, 2)
                    s_max(b, s)
                    recip(b, s - 1, 1)
                    ln_stats(b, s - 2, not prev)

            setup()
            dve.wait_ge(su_filled, N_SETUP)
            dve.wait_ge(*evacuated(FILL_OF["kh", PAIRS - 1]))
            dve.wait_ge(pads_set, N_PADS)
            batch(0, False)
            with dve.Fori(1, NB) as b:
                batch(b, True)
            head(NB, True, False)

        @block.gpsimd
        def _(pool):
            g_ = nc.gpsimd

            def f_bias(b, s):
                pool.wait_ge(f_loaded[s % SLOTS], 16 * ((TILES // SLOTS) * b + s // SLOTS + 1))
                if s == 0:
                    pool.wait_ge(rb_loaded, 16 * (b + 1))
                g_.tensor_tensor(f_slot(s), f_slot(s), rb1[:, :], ALU.add).then_inc(f_biased, 1)

            def normalise(b, s, half):
                h0, h1 = HALVES[half]
                pool.wait_ge(rsum_ready, 2 * (b * TILES + s) + half + 1)
                p = f_slot(s, h0 * KEYS, h1 * KEYS).rearrange("p (h n) -> p h n", n=KEYS)
                g_.tensor_tensor(p, p, rsum[:, s % 2, h0:h1].unsqueeze(2).broadcast_to([P, h1 - h0, KEYS]), ALU.mult).then_inc(probs_ready, 1)

            def normalise0(b, g):
                pool.wait_ge(rsum0_ready, b * GROUPS + g + 1)
                e = attn[:, g * GROUP * P:(g + 1) * GROUP * P].rearrange("p (i n) -> p i n", i=GROUP)[:, :, 0:KEYS]
                g_.tensor_tensor(e, e, rsum0[:, g * GROUP:(g + 1) * GROUP].unsqueeze(2).broadcast_to([P, GROUP, KEYS]),
                                 ALU.mult).then_inc(attn_ready, 1)

            def x1(b, i):
                for g, (t0, _) in enumerate(X_PIECES):
                    if i == t0:
                        pool.wait_ge(x_loaded[g], 16 * (b + 1))
                pool.wait_ge(gated, b * TILES + i + 1)
                xt = xrow[:, i * D:(i + 1) * D]
                g_.tensor_tensor(xt, xt, o_sb[:, i % 2, :], ALU.add).then_inc(x1_ready, 1)

            def rstd_of(b, s):
                pool.wait_ge(var_ready, b * TILES + s + 1)
                j = s % YSLOTS
                g_.tensor_tensor(rstd[:, j:j + 1], var_eps[:, j:j + 1], small[:, 1:2], ALU.pow).then_inc(rstd_ready, 1)

            def ln_affine(b, s):
                yt = y[:, s % YSLOTS, :]
                pool.wait_ge(y_normed, b * TILES + s + 1)
                g_.tensor_tensor(yt, yt, ln_gb[:, 0, :], ALU.mult).then_inc(y_scaled, 1)
                pool.wait_ge(y_scaled, b * TILES + s + 1)
                g_.tensor_tensor(yt, yt, ln_gb[:, 1, :], ALU.add).then_inc(y_final, 1)

            def head(b, prev, cur):
                if prev:
                    rstd_of(b - 1, 5)
                if cur:
                    normalise0(b, 0)
                if prev:
                    normalise(b - 1, 7, 0)
                if cur:
                    normalise0(b, 1)
                    if prev:
                        f_bias(b, 0)
                if prev:
                    normalise(b - 1, 7, 1)
                    ln_affine(b - 1, 5)
                    rstd_of(b - 1, 6)
                if cur:
                    for i in range(TILES):
                        x1(b, i)
                        if i == 1 and prev:
                            ln_affine(b - 1, 6)
                        if i == 4 and prev:
                            rstd_of(b - 1, 7)
                        if i == 7 and not prev:
                            f_bias(b, 0)
                else:
                    ln_affine(b - 1, 6)
                    rstd_of(b - 1, 7)

            def batch(b, prev):
                head(b, prev, True)
                for s in range(TILES):
                    if s > 2:
                        rstd_of(b, s - 3)
                    if s + 1 < TILES:
                        f_bias(b, s + 1)
                    if s == 1 and prev:
                        ln_affine(b - 1, 7)
                    if s:
                        normalise(b, s - 1, 0)
                        normalise(b, s - 1, 1)
                    if s > 2:
                        ln_affine(b, s - 3)

            g_.memset(warm, 0.0).then_inc(warm_ready, 1)
            g_.memset(bq_blk[:, :], 0.0).then_inc(pads_set, 1)
            g_.memset(small[:, 1:2], -0.5).then_inc(pads_set, 1)
            g_.memset(vvs_hi[:, :].bitcast(F32), 0.0).then_inc(pads_set, 1)
            g_.memset(vvs_lo[:, :].bitcast(F32), 0.0).then_inc(pads_set, 1)
            g_.memset(m_all[:, :, AK:], 0.0).then_inc(pads_set, 1)
            g_.memset(fs_slots[:, :, HK:], 0.0).then_inc(pool_chain, 1)
            pool.wait_ge(pool_chain, 1)
            g_.memset(fs_slots[:, :, (CH - 1) * P + ONE_ROW:(CH - 1) * P + ONE_ROW + 1], 1.0).then_inc(pads_set, 1)
            for part in (blk_v_hi, blk_v_lo):
                g_.memset(part[:, :].bitcast(F32), 0.0).then_inc(pads_set, 1)
            for i, (raw, hi, lo) in enumerate(((wk_sb, wk_hi, wk_lo), (wv_sb, wv_hi, wv_lo))):
                for j, (a, e) in enumerate(W_HALVES):
                    pool.wait_ge(w_hi_ready, 2 * i + j + 1)
                    g_.tensor_tensor(lo[:, :, a:e], raw[:, :, a:e], hi[:, :, a:e], ALU.subtract).then_inc(w_lo_ready, 1)
            pool.wait_ge(su_filled, VVS_DONE)
            pool.wait_ge(vvs_lo_ready, NB)
            g_.memset(blk_k[:, :], 0.0).then_inc(pads_set, 1)
            g_.memset(attn[:, :].rearrange("p (i n) -> p i n", i=TILES)[:, :, KEYS:], 0.0).then_inc(pads_set, 1)
            pool.wait_ge(wo_hi_ready, 1)
            g_.tensor_tensor(wo_lo[:, :, :].rearrange("p (c k) n -> p c (k n)", c=DC), wo_raw,
                             wo_hi[:, :, :].rearrange("p (c k) n -> p c (k n)", c=DC), ALU.subtract).then_inc(wo_lo_ready, 1)
            batch(0, False)
            with pool.Fori(1, NB) as b:
                batch(b, True)
            head(NB, True, False)


_OUT = (NB, SEQ, D)


def kernel(**inputs):
    import numpy as np
    import concourse.bacc as bacc
    from concourse.bass_utils import run_bass_kernel_spmd

    a = {k: np.asarray(v) for k, v in inputs.items()}
    l0 = {k[9:]: v for k, v in a.items() if k.startswith("L0_xattn_")}
    l1 = {k[9:]: v for k, v in a.items() if k.startswith("L1_xattn_")}
    x = a["x"].reshape(NB * SEQ, D)
    chunks = [v.reshape(-1, P).T for v in (l0["bk"], l0["bv"], l0["bq"], l1["bq"], l1["bk"], l1["bv"])]
    arrays = {
        "x": x, "xT": x.T, "cT": a["ctx_1024"].reshape(AK, D).T,
        "fside": a["fside_Bx16xSxS2_0"].transpose(0, 2, 1, 3).reshape(NB * SEQ, HK),
        "wq0": l0["Wq"], "wk0T": l0["Wk"].T, "wv0T": l0["Wv"].T,
        "w1T": l0["W1"].T, "w2T": l0["W2"].T, "w3T": l0["W3"].T,
        "wqT": l1["wq"].T, "wk": l1["wk"], "wv": l1["wv"], "wo": l1["wo"],
        "cols": np.concatenate(chunks, axis=1),
        "rows": np.stack([l0["b1"], l0["b2"], l0["b3"], l1["ln_g"], l1["ln_b"]]),
        "bo": l1["bo"].reshape(1, D), "gamma": l0["gamma"].reshape(1), "ident_in": np.eye(P, dtype=np.float32),
    }
    arrays = {f"in_{k}": np.ascontiguousarray(v) for k, v in arrays.items()}
    nc = bacc.Bacc("TRN2", target_bir_lowering=False, num_devices=1)
    args = [nc.dram_tensor(k, v.shape, mybir.dt.from_np(v.dtype), kind="ExternalInput").ap() for k, v in arrays.items()]
    args.append(nc.dram_tensor("out_0", (NB * SEQ, D), F32, kind="ExternalOutput").ap())
    build(nc, *args, nc.dram_tensor("rb_rows", (NB, HK), F32, kind="Internal").ap(),
          nc.dram_tensor("vh_parts", (2, P, PAIRS * AK), F32, kind="Internal").ap())
    r = run_bass_kernel_spmd(nc, [arrays], core_ids=[0])
    return r.results[0]["out_0"].reshape(_OUT)
```
